# Optimizing a Trainium2 kernel written in Bass

```python
import numpy as np
import jax
import jax.numpy as jnp

def _softmax(x, axis=-1):
    return jax.nn.softmax(x, axis=axis)

def _gelu(x):
    return jax.nn.gelu(x, approximate=True)

def _silu(x):
    return jax.nn.silu(x)

def _sigmoid(x):
    return jax.nn.sigmoid(x)

def _layernorm(x, axis=-1, eps=1e-05):
    m = jnp.mean(x, axis=axis, keepdims=True)
    v = jnp.var(x, axis=axis, keepdims=True)
    return (x - m) / jnp.sqrt(v + eps)

def _scatter_add(tgt, idx, src, axis=0):
    return tgt.at[idx].add(src)

def _segment_sum(src, seg, n):
    return jax.ops.segment_sum(src, seg, n)
kernel_name = 'mk_metaformer_d1_conv_nchw128_r2_22f4ad'

def setup_inputs(seed: int=0):
    np.random.seed(seed)
    _w = jnp.asarray

    def _rec_inputs():
        import jax
        import jax.numpy as jnp
        _gk = jax.random.key(seed)
        x = -0.0002091 + 1 * jax.random.normal(jax.random.fold_in(_gk, 1), (32, 64, 56, 56), jnp.float32)
        return x
    x = _rec_inputs()

    def _L0_conv_setup():
        import jax, jax.numpy as jnp
        import numpy as np
        BN_EPS = 1e-05

        def binary_activation(x):
            out_fwd = jnp.sign(x)
            m1 = (x < -1.0).astype(x.dtype)
            m2 = (x < 0.0).astype(x.dtype)
            m3 = (x < 1.0).astype(x.dtype)
            out1 = -1.0 * m1 + (x * x + 2.0 * x) * (1.0 - m1)
            out2 = out1 * m2 + (-x * x + 2.0 * x) * (1.0 - m2)
            out3 = out2 * m3 + 1.0 * (1.0 - m3)
            return jax.lax.stop_gradient(out_fwd - out3) + out3

        def binary_conv3x3(x, w, stride=1):
            scale = jax.lax.stop_gradient(jnp.mean(jnp.abs(w), axis=(1, 2, 3), keepdims=True))
            bw_no_grad = jax.lax.stop_gradient(scale * jnp.sign(w))
            cw = jnp.clip(w, -1.0, 1.0)
            bw = bw_no_grad - jax.lax.stop_gradient(cw) + cw
            return jax.lax.conv_general_dilated(x, bw, window_strides=(stride, stride), padding=[(1, 1), (1, 1)], dimension_numbers=('NCHW', 'OIHW', 'NCHW'))

        def batchnorm_inference(y, gamma, beta, mean, var):
            inv = gamma * jax.lax.rsqrt(var + BN_EPS)
            return y * inv[None, :, None, None] + (beta - mean * inv)[None, :, None, None]
        key = jax.random.key(seed)
        k1, k2, k3 = jax.random.split(key, 3)
        N, Cin, Cout, H, W = (32, 64, 64, 56, 56)
        x = jax.random.normal(k1, (N, Cin, H, W), dtype=jnp.float32)
        weight = jax.random.normal(k2, (Cout, Cin, 3, 3), dtype=jnp.float32) * 0.1
        gamma = jnp.ones((Cout,), dtype=jnp.float32)
        beta = jnp.zeros((Cout,), dtype=jnp.float32)
        bn_mean = jnp.zeros((Cout,), dtype=jnp.float32)
        bn_var = jax.random.uniform(k3, (Cout,), dtype=jnp.float32)
        return {'x': x, 'weight': weight, 'gamma': gamma, 'beta': beta, 'bn_mean': bn_mean, 'bn_var': bn_var}
    _L0_conv_all = _L0_conv_setup()
    _L0_conv_in = {k: v for k, v in _L0_conv_all.items() if k in ('weight', 'gamma', 'beta', 'bn_mean', 'bn_var')}
    del _L0_conv_all

    def _L0_ffn_setup():
        import jax, jax.numpy as jnp
        import numpy as np
        PADDED_SL = 4096
        TEMPERATURE = 1.0
        SIGMA_POW = 0.25

        def _stu_conv(phi, u, n):
            b, sl, d = u.shape
            sgn = jnp.where(jnp.arange(sl) % 2 == 0, 1.0, -1.0).astype(u.dtype)
            sgn3 = sgn[None, :, None]
            Vf = jnp.fft.rfft(phi, n=n, axis=0)
            Uf_p = jnp.fft.rfft(u, n=n, axis=1)
            Uf_m = jnp.fft.rfft(u * sgn3, n=n, axis=1)
            U_plus = jnp.fft.irfft(Vf[None, :, :, None] * Uf_p[:, :, None, :], n=n, axis=1)[:, :sl]
            U_minus = jnp.fft.irfft(Vf[None, :, :, None] * Uf_m[:, :, None, :], n=n, axis=1)[:, :sl]
            U_minus = U_minus * sgn[None, :, None, None]
            return (U_plus, U_minus)

        def _compute_spectral(u, sigma, phi, Mpp, Mpm):
            U_plus, U_minus = _stu_conv(phi, u, PADDED_SL)
            s = sigma ** SIGMA_POW
            out = jnp.einsum('btkd,k,kde->bte', U_plus, s, Mpp)
            out = out + jnp.einsum('btkd,k,kde->bte', U_minus, s, Mpm)
            return out

        def _compute_ar_u(Mu, u):
            sl = u.shape[1]
            out = jnp.zeros(u.shape[:2] + (Mu.shape[-1],), dtype=u.dtype)
            for i in range(Mu.shape[0]):
                ui = jnp.pad(u, ((0, 0), (i, 0), (0, 0)))[:, :sl]
                out = out + jnp.einsum('btd,de->bte', ui, Mu[i])
            return out

        def _stu(u, sigma, phi, Mu, Mpp, Mpm):
            return _compute_spectral(u, sigma, phi, Mpp, Mpm) + _compute_ar_u(Mu, u)
        key = jax.random.key(seed)
        ks = jax.random.split(key, 8)
        b, sl, d, K, k_u = (2, 2048, 64, 16, 3)
        x = jax.random.normal(ks[0], (b, sl, d), dtype=jnp.float32)
        sigma = jax.random.uniform(ks[1], (K,), dtype=jnp.float32, minval=0.001, maxval=1.0)
        phi = jax.random.normal(ks[2], (sl, K), dtype=jnp.float32) / np.sqrt(sl)
        M_u = jax.random.normal(ks[3], (4, k_u, d, d), dtype=jnp.float32) * 0.02
        M_phi_plus = jax.random.normal(ks[4], (4, K, d, d), dtype=jnp.float32) * 0.02
        M_phi_minus = jax.random.normal(ks[5], (4, K, d, d), dtype=jnp.float32) * 0.02
        log_weights = jnp.ones((4,), dtype=jnp.float32)
        u01 = jax.random.uniform(ks[6], (4,), dtype=jnp.float32, minval=1e-06, maxval=1.0 - 1e-06)
        gumbel = -jnp.log(-jnp.log(u01))
        return {'x': x, 'sigma': sigma, 'phi': phi, 'M_u': M_u, 'M_phi_plus': M_phi_plus, 'M_phi_minus': M_phi_minus, 'log_weights': log_weights, 'gumbel': gumbel}
    _L0_ffn_all = _L0_ffn_setup()
    _L0_ffn_in = {k: v for k, v in _L0_ffn_all.items() if k in ('sigma', 'phi', 'M_u', 'M_phi_plus', 'M_phi_minus', 'log_weights', 'gumbel')}
    del _L0_ffn_all
    return {'x': x, 'L0_conv_weight': _L0_conv_in['weight'], 'L0_conv_gamma': _L0_conv_in['gamma'], 'L0_conv_beta': _L0_conv_in['beta'], 'L0_conv_bn_mean': _L0_conv_in['bn_mean'], 'L0_conv_bn_var': _L0_conv_in['bn_var'], 'L0_ffn_sigma': _L0_ffn_in['sigma'], 'L0_ffn_phi': _L0_ffn_in['phi'], 'L0_ffn_M_u': _L0_ffn_in['M_u'], 'L0_ffn_M_phi_plus': _L0_ffn_in['M_phi_plus'], 'L0_ffn_M_phi_minus': _L0_ffn_in['M_phi_minus'], 'L0_ffn_log_weights': _L0_ffn_in['log_weights'], 'L0_ffn_gumbel': _L0_ffn_in['gumbel']}

def reference(x, L0_conv_weight, L0_conv_gamma, L0_conv_beta, L0_conv_bn_mean, L0_conv_bn_var, L0_ffn_sigma, L0_ffn_phi, L0_ffn_M_u, L0_ffn_M_phi_plus, L0_ffn_M_phi_minus, L0_ffn_log_weights, L0_ffn_gumbel):
    import jax
    import jax.numpy as jnp

    def _L0_conv_ref(x, weight, gamma, beta, bn_mean, bn_var):
        import jax, jax.numpy as jnp
        import numpy as np
        BN_EPS = 1e-05

        def binary_activation(x):
            out_fwd = jnp.sign(x)
            m1 = (x < -1.0).astype(x.dtype)
            m2 = (x < 0.0).astype(x.dtype)
            m3 = (x < 1.0).astype(x.dtype)
            out1 = -1.0 * m1 + (x * x + 2.0 * x) * (1.0 - m1)
            out2 = out1 * m2 + (-x * x + 2.0 * x) * (1.0 - m2)
            out3 = out2 * m3 + 1.0 * (1.0 - m3)
            return jax.lax.stop_gradient(out_fwd - out3) + out3

        def binary_conv3x3(x, w, stride=1):
            scale = jax.lax.stop_gradient(jnp.mean(jnp.abs(w), axis=(1, 2, 3), keepdims=True))
            bw_no_grad = jax.lax.stop_gradient(scale * jnp.sign(w))
            cw = jnp.clip(w, -1.0, 1.0)
            bw = bw_no_grad - jax.lax.stop_gradient(cw) + cw
            return jax.lax.conv_general_dilated(x, bw, window_strides=(stride, stride), padding=[(1, 1), (1, 1)], dimension_numbers=('NCHW', 'OIHW', 'NCHW'))

        def batchnorm_inference(y, gamma, beta, mean, var):
            inv = gamma * jax.lax.rsqrt(var + BN_EPS)
            return y * inv[None, :, None, None] + (beta - mean * inv)[None, :, None, None]
        residual = x
        out = binary_activation(x)
        out = binary_conv3x3(out, weight, stride=1)
        out = batchnorm_inference(out, gamma, beta, bn_mean, bn_var)
        return out + residual

    def _L0_ffn_ref(x, sigma, phi, M_u, M_phi_plus, M_phi_minus, log_weights, gumbel):
        import jax, jax.numpy as jnp
        import numpy as np
        PADDED_SL = 4096
        TEMPERATURE = 1.0
        SIGMA_POW = 0.25

        def _stu_conv(phi, u, n):
            b, sl, d = u.shape
            sgn = jnp.where(jnp.arange(sl) % 2 == 0, 1.0, -1.0).astype(u.dtype)
            sgn3 = sgn[None, :, None]
            Vf = jnp.fft.rfft(phi, n=n, axis=0)
            Uf_p = jnp.fft.rfft(u, n=n, axis=1)
            Uf_m = jnp.fft.rfft(u * sgn3, n=n, axis=1)
            U_plus = jnp.fft.irfft(Vf[None, :, :, None] * Uf_p[:, :, None, :], n=n, axis=1)[:, :sl]
            U_minus = jnp.fft.irfft(Vf[None, :, :, None] * Uf_m[:, :, None, :], n=n, axis=1)[:, :sl]
            U_minus = U_minus * sgn[None, :, None, None]
            return (U_plus, U_minus)

        def _compute_spectral(u, sigma, phi, Mpp, Mpm):
            U_plus, U_minus = _stu_conv(phi, u, PADDED_SL)
            s = sigma ** SIGMA_POW
            out = jnp.einsum('btkd,k,kde->bte', U_plus, s, Mpp)
            out = out + jnp.einsum('btkd,k,kde->bte', U_minus, s, Mpm)
            return out

        def _compute_ar_u(Mu, u):
            sl = u.shape[1]
            out = jnp.zeros(u.shape[:2] + (Mu.shape[-1],), dtype=u.dtype)
            for i in range(Mu.shape[0]):
                ui = jnp.pad(u, ((0, 0), (i, 0), (0, 0)))[:, :sl]
                out = out + jnp.einsum('btd,de->bte', ui, Mu[i])
            return out

        def _stu(u, sigma, phi, Mu, Mpp, Mpm):
            return _compute_spectral(u, sigma, phi, Mpp, Mpm) + _compute_ar_u(Mu, u)
        T = x.shape[1]
        outs = []
        for i, frac in enumerate((1, 2, 4, 8)):
            xi = x[:, :T // frac]
            si = _stu(xi, sigma, phi, M_u[i], M_phi_plus[i], M_phi_minus[i])
            si = jnp.pad(si, ((0, 0), (0, T - si.shape[1]), (0, 0)))
            outs.append(si)
        y_soft = jax.nn.softmax((log_weights + gumbel) / TEMPERATURE)
        y_hard = jax.nn.one_hot(jnp.argmax(y_soft), 4, dtype=y_soft.dtype)
        weights = y_hard - jax.lax.stop_gradient(y_soft) + y_soft
        stacked = jnp.stack(outs, axis=-1)
        return jnp.sum(stacked * weights, axis=-1)

    def _gn(v, G=32, eps=1e-05):
        B_, C_, H_, W_ = v.shape
        g = v.reshape(B_, G, C_ // G, H_, W_)
        m = jnp.mean(g, axis=(2, 3, 4), keepdims=True)
        s = jnp.var(g, axis=(2, 3, 4), keepdims=True)
        return ((g - m) / jnp.sqrt(s + eps)).reshape(v.shape)

    def _ln_c(v, eps=1e-06):
        m = jnp.mean(v, axis=1, keepdims=True)
        s = jnp.var(v, axis=1, keepdims=True)
        return (v - m) / jnp.sqrt(s + eps)

    def _ln_t(v, eps=1e-05):
        m = jnp.mean(v, axis=-1, keepdims=True)
        s = jnp.var(v, axis=-1, keepdims=True)
        return (v - m) / jnp.sqrt(s + eps)

    def _to_tokens(v):
        B_, C_, H_, W_ = v.shape
        return v.reshape(B_, C_, H_ * W_).transpose(0, 2, 1)

    def _from_tokens(t, like):
        B_, C_, H_, W_ = like.shape
        return t.transpose(0, 2, 1).reshape(B_, C_, H_, W_)
    x = x + _L0_conv_ref(_ln_c(x), L0_conv_weight, L0_conv_gamma, L0_conv_beta, L0_conv_bn_mean, L0_conv_bn_var)
    t = _to_tokens(x)
    t = t + _L0_ffn_ref(_ln_t(t), L0_ffn_sigma, L0_ffn_phi, L0_ffn_M_u, L0_ffn_M_phi_plus, L0_ffn_M_phi_minus, L0_ffn_log_weights, L0_ffn_gumbel)
    x = _from_tokens(t, x)
    return x

_drawn_inputs = setup_inputs


def setup_inputs(seed=0):
    import zlib

    import numpy as np

    out = dict(_drawn_inputs(seed))
    spreads = {'L0_conv_gamma': (1.0, 0.2),
     'L0_conv_beta': (0.0, 0.309),
     'L0_conv_bn_mean': (0.0, 0.1),
     'L0_ffn_log_weights': (1.0, 0.2)}
    factors = {}
    for name, (base, spread) in spreads.items():
        noise = np.random.default_rng([zlib.crc32(name.encode()), seed]).standard_normal(out[name].shape)
        drawn = base * np.exp(spread * noise) if base else spread * noise
        out[name] = jnp.asarray(drawn.astype(out[name].dtype))
    for name, factor in factors.items():
        out[name] = (out[name] * factor).astype(out[name].dtype)
    return out
```

```python
from contextlib import ExitStack

import numpy as np

import concourse.bass as bass
from concourse import mybir

F32 = mybir.dt.float32
BF16 = mybir.dt.bfloat16
I32 = mybir.dt.int32
ALU = mybir.AluOpType
ACT = mybir.ActivationFunctionType
AX = mybir.AxisListType.X

NIMG, CH, HGT, WID = 32, 64, 56, 56
TOK = HGT * WID
NBR = 4
KF, KU = 16, 3
PHI_LEN = 2048
NFFT = 4096

NA = 32
NB = TOK // NA
NSLOT = 64
NALPHA = 32
NROW = 2 * NSLOT
NUNIT = NSLOT // 2
NF = 2 * NALPHA
NK = 2 * KF + KU
KI = 64
KROWS = KI + NK
NPAIR = NIMG // 2
ZCOLS = NIMG * CH + NK

CROWS = 8
NCONV = HGT // CROWS
CW = CROWS * WID
ACH = 4
NTOK = NA // ACH
TW = ACH * 2 * CH
MASKG = 8
NMASK = NA // MASKG

RSQRT_MAGIC = 0x5F3759DF
NEWTON = 3


def slot_frequencies(s):
    if s:
        return [s + 128 * al for al in range(NALPHA)]
    return [128 * al for al in range(16)] + [64 + 128 * al for al in range(16)]


def constants():
    b = np.arange(NB)
    s1 = np.zeros((NB, NROW))
    s2 = np.zeros((NROW, NB))
    s1[:, 0], s1[:, 1] = 1.0, (-1.0) ** b
    s2[0], s2[1] = 1.0, (-1.0) ** b
    for s in range(1, NSLOT):
        th = 2 * np.pi * s * b / 128
        s1[:, 2 * s], s1[:, 2 * s + 1] = np.cos(th), -np.sin(th)
        s2[2 * s], s2[2 * s + 1] = np.cos(th), -np.sin(th)

    a = np.arange(NA)[:, None]
    fwd = np.zeros((NUNIT, 2, 2, NA, 3, 2, 2, NALPHA))
    inv = np.zeros((NUNIT, 2, 2, 2, NALPHA, NA))
    for s in range(NSLOT):
        u, sl = divmod(s, 2)
        f = np.array(slot_frequencies(s))[None, :]
        th = 2 * np.pi * f * a / NFFT
        c, sn = np.cos(th), np.sin(th)
        re_re, re_im, im_re, im_im = c.copy(), -sn, sn.copy(), c.copy()
        ci, si = 2 * c.T / NFFT, 2 * sn.T / NFFT
        g = np.array([[ci, si], [-si, ci]])
        if s == 0:
            z = np.zeros((NA, 16))
            re_re = np.hstack([c[:, :16], z])
            re_im = np.hstack([-sn[:, :16], z])
            im_re = np.hstack([z, c[:, 16:]])
            im_im = np.hstack([z, -sn[:, 16:]])
            re_im[:, 0] = (-1.0) ** a[:, 0]
            g[:] = 0.0
            g[0, 0, :16], g[1, 0, :16] = ci[:16], -si[:16]
            g[0, 1, 16:], g[1, 1, 16:] = ci[16:], -si[16:]
            g[0, 0, 0] = 1.0 / NFFT
            g[1, 0, 0] = (-1.0) ** a[:, 0] / NFFT
        x = np.array([[re_re, re_im], [im_re, im_im]])
        first, second = x.copy(), np.stack([x[:, 1], -x[:, 0]], 1)
        if s == 0:
            first[:, 1, :, 0] = 0.0
            second[:, 0, :, 0] = 0.0
            second[:, 1, :, 0] = -x[:, 1, :, 0]
        for n, m in enumerate((x, first, second)):
            fwd[u, sl, :, :, n, :, sl] = m.transpose(0, 2, 1, 3)
        inv[u, sl] = g
    fwd = fwd.reshape(NUNIT, 128, 3 * 128)
    ib = np.zeros((NUNIT, 2, 2, NALPHA, 2, 2, 2, 2, NA))
    for h in range(2):
        for sl in range(2):
            ib[:, h, sl, :, :, :, h, sl, :] = inv[:, sl].transpose(0, 3, 1, 2, 4)
    inv = ib.reshape(NUNIT, 128, 4 * 128)

    center = np.kron(np.eye(2), np.eye(CH) - 1.0 / CH)
    t = (np.arange(NMASK) * MASKG)[None, :] + NA * b[:, None]
    mask = np.stack([t < (TOK >> i) for i in range(NBR)], -1)
    mask_col = mask.reshape(NB, NMASK * NBR)
    mask_row = np.broadcast_to(mask.transpose(1, 2, 0).reshape(1, -1), (128, NMASK * NBR * NB))
    sign_a = np.broadcast_to((-1.0) ** np.arange(NA), (KI, NA))
    out = {
        "c_step1": s1, "c_step_last": s2, "c_fwd": fwd, "c_inv": inv, "c_center": center,
        "c_ident": np.eye(128), "c_mask_col": mask_col, "c_mask_row": mask_row, "c_sign_a": sign_a,
    }
    return {k: np.ascontiguousarray(v, dtype=np.float32) for k, v in out.items()}


def rsqrt_steps(nc, link, y, v, t0, t1):
    link(nc.vector.tensor_scalar(t0.bitcast(I32), v.bitcast(I32), 1, None, ALU.logical_shift_right))
    link(nc.vector.tensor_scalar(y.bitcast(I32), t0.bitcast(I32), -1.0, float(RSQRT_MAGIC), ALU.mult, ALU.add))
    for _ in range(NEWTON):
        link(nc.vector.tensor_tensor(t0, y, y, ALU.mult))
        link(nc.vector.scalar_tensor_tensor(t1, t0, -0.5, v, ALU.mult, ALU.mult))
        link(nc.vector.scalar_tensor_tensor(y, t1, 1.5, y, ALU.add, ALU.mult))


RSQRT_STEPS = 2 + 3 * NEWTON


def two_by_two(eng, count, body):
    body(0, 0, 1)
    with eng.Fori(0, (count - 2) // 2) as h:
        body(2 * h + 1, 1, h + 1)
        body(2 * h + 2, 0, h + 2)
    body(count - 1, (count - 1) % 2, (count - 1) // 2 + 1)


def after_wait(eng, sem):
    eng.sem_inc(sem, 1)


def is_first(n):
    return isinstance(n, int) and n == 0


def prepare(nc, ctx, d, keep):
    with ExitStack() as own:
        def sb(name, shape, dt=F32):
            return own.enter_context(nc.sbuf_tensor(name, shape, dt))

        def sem(name):
            return own.enter_context(nc.semaphore(name))

        w_raw = sb("w_raw", [128, CH * 9])
        w_diag = sb("w_diag", [128, 9, 128])
        bn = sb("bn", [128, 16])
        mix = sb("mix", [128, 64])
        s1 = sb("s1", [NB, NROW])
        s2 = sb("s2", [NROW, NB])
        mask_col = sb("mask_col", [NB, NMASK * NBR])
        mask_row = sb("mask_row", [128, NMASK, NBR, NB])
        mask_cs = sb("mask_cs", [NB, NMASK])
        mask_rs = sb("mask_rs", [128, NMASK, NB])
        sgn_a = sb("sgn_a", [KI, NA])
        phi = sb("phi", [KI, NA, KF])
        sig = sb("sig", [KI, 3, KF])
        filt = sb("filt", [KI, NA, NK])
        filt_z = sb("filt_z", [NROW, NA, NK])
        m_raw = sb("m_raw", [KROWS, 2, CH * CH])
        m_acc = sb("m_acc", [KROWS, CH * CH])
        p_w = own.enter_context(nc.psum_tensor("p_w", [128, 4, 512], F32))
        p_f = own.enter_context(nc.psum_tensor("p_f", [128, 4, 512], F32))

        loaded = {n: sem("loaded_" + n) for n in ("conv", "bn", "mix", "mask", "phi", "const")}
        m_loaded = [sem(f"m_loaded{i}") for i in range(2)]
        zeroed, signed, turned = sem("zeroed"), sem("signed"), sem("turned")
        m_zeroed, pow_done, exp_in, exp_done = sem("m_zeroed"), sem("pow_done"), sem("exp_in"), sem("exp_done")
        step, m_used, filt_ready, filt_dft, filt_saved, filt_stored = (
            sem(n) for n in ("prep_step", "m_used", "filt_ready", "filt_dft", "filt_saved", "filt_stored"))

        block = own.enter_context(nc.Block())

        @block.sync
        def _(sp):
            for h in range(2):
                half = slice(CH * h, CH * h + CH)
                sp.dma_start(w_raw[half, :], d["weight"].rearrange("o i h w -> o (i h w)")).then_inc(loaded["conv"], 16)
                for n, name in enumerate(("gamma", "beta", "bn_mean", "bn_var")):
                    sp.dma_start(bn[half, n:n + 1], d[name].rearrange("(o a) -> o a", a=1)).then_inc(loaded["bn"], 16)
            sp.dma_start(keep["ident"][:], d["c_ident"]).then_inc(loaded["const"], 16)
            sp.dma_start(keep["center"][:], d["c_center"]).then_inc(loaded["const"], 16)
            sp.dma_start(phi[:], d["phi"].rearrange("(b a) k -> b a k", a=NA)).then_inc(loaded["phi"], 16)
            sp.dma_start(sig[:, 0, :], d["sigma"].partition_broadcast(KI)).then_inc(loaded["phi"], 16)
            sp.dma_start(sgn_a[:], d["c_sign_a"]).then_inc(loaded["phi"], 16)
            sp.dma_start(mix[:, 0:4], d["log_weights"].partition_broadcast(128)).then_inc(loaded["mix"], 16)
            sp.dma_start(mix[:, 4:8], d["gumbel"].partition_broadcast(128)).then_inc(loaded["mix"], 16)
            sp.dma_start(s1[:], d["c_step1"]).then_inc(loaded["mask"], 16)
            sp.dma_start(s2[:], d["c_step_last"]).then_inc(loaded["mask"], 16)
            sp.dma_start(mask_col[:], d["c_mask_col"]).then_inc(loaded["mask"], 16)
            sp.dma_start(mask_row[:].rearrange("p g i b -> p (g i b)"), d["c_mask_row"]).then_inc(loaded["mask"], 16)
            sp.wait_ge(m_zeroed, 1)
            for i in range(NBR):
                if i >= 2:
                    sp.wait_ge(m_used, i - 1)
                for at in (0, KI):
                    for row, n, src in ((0, KF, d["M_plus"]), (KF, KF, d["M_minus"]), (2 * KF, KU, d["M_u"])):
                        sp.dma_start(m_raw[at + row:at + row + n, i % 2, :],
                                     src[i].rearrange("k d e -> k (d e)")).then_inc(m_loaded[i % 2], 16)
            sp.wait_ge(filt_saved, 4)
            sp.dma_start(d["z"][:, :, NIMG * CH:ZCOLS], filt_z[:]).then_inc(filt_stored, 16)
            sp.wait_ge(filt_stored, 16)

        @block.gpsimd
        def _(pool):
            nc.gpsimd.memset(m_raw[:], 0.0).then_inc(m_zeroed, 1)
            nc.gpsimd.memset(sig[:, 1, :], 0.25).then_inc(zeroed, 1)
            pool.wait_ge(zeroed, 1)
            pool.wait_ge(loaded["phi"], 48)
            nc.gpsimd.tensor_tensor(sig[:, 2, :], sig[:, 0, :], sig[:, 1, :], ALU.pow).then_inc(pow_done, 1)
            nc.gpsimd.memset(keep["mt"][:], 0.0).then_inc(m_zeroed, 1)
            nc.gpsimd.memset(keep["pad"][:], 0.0).then_inc(m_zeroed, 1)
            nc.gpsimd.memset(keep["vmov"][:], 0.0).then_inc(m_zeroed, 1)

        @block.scalar
        def _(act):
            act.wait_ge(loaded["conv"], 32)
            act.wait_ge(step, 1)
            for h in range(2):
                half = slice(CH * h, CH * h + CH)
                nc.scalar.activation(w_diag[half, :, half], w_raw[half, :].rearrange("o (i t) -> o t i", t=9),
                                     ACT.Sign).then_inc(signed, 1)
            act.wait_ge(exp_in, 1)
            nc.scalar.activation(mix[:, 12:16], mix[:, 12:16], ACT.Exp).then_inc(exp_done, 1)

        @block.tensor
        def _(pe):
            pe.wait_ge(loaded["const"], 32)
            pe.wait_ge(signed, 2)
            for t in range(9):
                mm = nc.tensor.transpose(p_w[:, t // 4, 128 * (t % 4):128 * (t % 4) + 128], w_diag[:, t, :],
                                         keep["ident"][:])
            mm.then_inc(turned, 1)
            pe.wait_ge(filt_ready, 1)
            for c in range(4):
                nc.tensor.matmul(p_f[:, c, 0:8 * NK], s1[0:KI, :], filt[:, 8 * c:8 * c + 8, :],
                                 start=True, stop=True).then_inc(filt_dft, 1)

        @block.vector
        def _(dve):
            n = [0]

            def link(ins):
                n[0] += 1
                ins.then_inc(step, 1)
                dve.wait_ge(step, n[0])

            link(nc.vector.memset(w_diag[:], 0.0))
            link(nc.vector.memset(filt[:], 0.0))
            for k in range(KU):
                link(nc.vector.memset(filt[0:1, k, 2 * KF + k:2 * KF + k + 1], 1.0))
            dve.wait_ge(pow_done, 1)
            link(nc.vector.tensor_tensor(filt[:, :, 0:KF], phi[:], sig[:, 2:3, :].to_broadcast([KI, NA, KF]), ALU.mult))
            link(nc.vector.tensor_tensor(filt[:, :, KF:2 * KF], filt[:, :, 0:KF],
                                         sgn_a[:].unsqueeze(2).to_broadcast([KI, NA, KF]), ALU.mult))
            dve.wait_ge(loaded["mask"], 64)
            nc.vector.memset(bn[:, 15:16], 0.0).then_inc(filt_ready, 1)

            dve.wait_ge(loaded["bn"], 128)
            dve.wait_ge(loaded["conv"], 32)
            link(nc.vector.tensor_reduce(bn[:, 4:5], w_raw[:], AX, ALU.add, apply_absolute_value=True))
            link(nc.vector.tensor_scalar(bn[:, 5:6], bn[:, 3:4], 1e-5, None, ALU.add))
            rsqrt_steps(nc, link, bn[:, 6:7], bn[:, 5:6], bn[:, 7:8], bn[:, 8:9])
            link(nc.vector.tensor_tensor(bn[:, 9:10], bn[:, 6:7], bn[:, 0:1], ALU.mult))
            link(nc.vector.scalar_tensor_tensor(keep["bn"][:, 0:1], bn[:, 4:5], 1.0 / (9 * CH), bn[:, 9:10],
                                                ALU.mult, ALU.mult))
            link(nc.vector.tensor_tensor(bn[:, 10:11], bn[:, 2:3], bn[:, 9:10], ALU.mult))
            link(nc.vector.tensor_tensor(keep["bn"][:, 1:2], bn[:, 1:2], bn[:, 10:11], ALU.subtract))
            dve.wait_ge(turned, 1)
            link(nc.vector.tensor_copy(keep["conv_w"][:].rearrange("p t o -> p (t o)"),
                                       p_w[:, 0:3, :].rearrange("p a b -> p (a b)")[:, 0:9 * 128]))

            dve.wait_ge(loaded["mix"], 32)
            link(nc.vector.tensor_tensor(mix[:, 8:12], mix[:, 0:4], mix[:, 4:8], ALU.add))
            link(nc.vector.tensor_reduce(mix[:, 16:17], mix[:, 8:12], AX, ALU.max))
            nc.vector.tensor_scalar(mix[:, 12:16], mix[:, 8:12], mix[:, 16:17], None, ALU.subtract).then_inc(exp_in, 1)
            dve.wait_ge(exp_done, 1)
            link(nc.vector.tensor_reduce(mix[:, 17:18], mix[:, 12:16], AX, ALU.add))
            link(nc.vector.reciprocal(mix[:, 18:19], mix[:, 17:18]))
            link(nc.vector.tensor_scalar(mix[:, 20:24], mix[:, 12:16], mix[:, 18:19], None, ALU.mult))
            link(nc.vector.tensor_reduce(mix[:, 19:20], mix[:, 20:24], AX, ALU.max))
            link(nc.vector.tensor_scalar(mix[:, 24:28], mix[:, 20:24], mix[:, 19:20], None, ALU.is_ge))
            link(nc.vector.tensor_scalar(mix[:, 28:32], mix[:, 24:28], -1.0, 1.0, ALU.mult, ALU.add))
            hard, soft, weight = mix[:, 32:36], mix[:, 20:24], mix[:, 36:40]
            link(nc.vector.tensor_copy(mix[:, 32:36], mix[:, 24:28]))
            for i in range(1, NBR):
                for j in range(i):
                    link(nc.vector.tensor_tensor(mix[:, 32 + i:33 + i], mix[:, 32 + i:33 + i], mix[:, 28 + j:29 + j],
                                                 ALU.mult))
            link(nc.vector.tensor_tensor(mix[:, 40:44], hard, soft, ALU.subtract))
            link(nc.vector.tensor_tensor(weight, mix[:, 40:44], soft, ALU.add))

            for i in range(NBR):
                mc = mask_col[:].rearrange("b (g i) -> b g i", i=NBR)[:, :, i]
                if i == 0:
                    link(nc.vector.tensor_scalar(mask_cs[:], mc, hard[0:NB, 0:1], None, ALU.mult))
                    link(nc.vector.tensor_scalar(mask_rs[:], mask_row[:, :, 0, :], hard[:, 0:1], None, ALU.mult))
                else:
                    link(nc.vector.scalar_tensor_tensor(mask_cs[:], mc, hard[0:NB, i:i + 1], mask_cs[:],
                                                        ALU.mult, ALU.add))
                    link(nc.vector.scalar_tensor_tensor(mask_rs[:], mask_row[:, :, i, :], hard[:, i:i + 1], mask_rs[:],
                                                        ALU.mult, ALU.add))
            for g in range(NMASK):
                link(nc.vector.tensor_scalar(keep["step1"][:, g, :], s1[:], mask_cs[:, g:g + 1], None, ALU.mult))
                link(nc.vector.tensor_tensor(keep["last"][:, g, :], s2[:], mask_rs[:, g, :], ALU.mult))

            for c in range(4):
                dve.wait_ge(filt_dft, c + 1)
                nc.vector.tensor_copy(filt_z[:, 8 * c:8 * c + 8, :].rearrange("p a k -> p (a k)"),
                                      p_f[:, c, 0:8 * NK]).then_inc(filt_saved, 1)

            for i in range(NBR):
                dve.wait_ge(m_loaded[i % 2], 96 * (i // 2 + 1))
                if i == 0:
                    ins = nc.vector.tensor_scalar(m_acc[:], m_raw[:, 0, :], weight[0:KROWS, 0:1], None, ALU.mult)
                else:
                    dve.wait_ge(m_used, i)
                    ins = nc.vector.scalar_tensor_tensor(m_acc[:], m_raw[:, i % 2, :], weight[0:KROWS, i:i + 1],
                                                         m_acc[:], ALU.mult, ALU.add)
                ins.then_inc(m_used, 1)
            dve.wait_ge(m_used, NBR)
            dve.wait_ge(m_zeroed, 4)
            link(nc.vector.tensor_copy(keep["mt"][0:NK, :, 0:CH],
                                       m_acc[0:NK, :].rearrange("k (d e) -> k e d", e=CH)))
            link(nc.vector.tensor_scalar(keep["mt"][KI:KROWS, :, CH:2 * CH],
                                         m_acc[KI:KROWS, :].rearrange("k (d e) -> k e d", e=CH), -1.0, None, ALU.mult))


def norm_and_convolve(nc, d, keep):
    with ExitStack() as own:
        def sb(name, shape, dt=F32):
            return own.enter_context(nc.sbuf_tensor(name, shape, dt))

        def sem(name):
            return own.enter_context(nc.semaphore(name))

        x_in = [sb(f"x_in{i}", [128, TOK]) for i in range(2)]
        conv_y = sb("conv_y", [128, TOK])
        xc_t = sb("xc_t", [NB, NTOK, TW])
        sq1 = sb("sq1", [NB, 2, TW])
        x1_t = sb("x1_t", [NB, NTOK, TW])
        u_t = sb("u_t", [NB, NTOK, TW])
        sq2 = sb("sq2", [NB, NTOK, TW])
        z_sb = sb("z_sb", [NROW, NTOK, TW])
        st1 = sb("st1", [NB, 5, 64])
        st2 = sb("st2", [NB, 6, 64])
        pad = keep["pad"]

        p_cen = own.enter_context(nc.psum_tensor("p_cen", [128, 2, 512], F32))
        p_conv = own.enter_context(nc.psum_tensor("p_conv", [128, 2, 512], F32))
        p_xt = own.enter_context(nc.psum_tensor("p_xt", [128, 2, 512], F32))
        p_rt = own.enter_context(nc.psum_tensor("p_rt", [128, 2, 512], F32))

        x_loaded = [sem(f"x_loaded{i}") for i in range(2)]
        (cen_ready, conv_ready, xt_ready, rt_ready, z_ready, sign_done, xt_copied, xt_squared, z_saved, y_saved,
         r_done, sq2_done, u_done, ssq1_done, x1_done, u_centered, rstd2_done, x1_stored, z_stored, step) = (
            sem(n) for n in (
                "cen_ready", "conv_ready", "xt_ready", "rt_ready", "z_ready", "sign_done", "xt_copied", "xt_squared",
                "z_saved", "y_saved", "r_done", "sq2_done", "u_done", "ssq1_done", "x1_done", "u_centered",
                "rstd2_done", "x1_stored", "z_stored", "norm_step"))
        sp_turn = sem("sp_turn")

        x_pairs = d["x"].rearrange("(q i) c h w -> q (i c) (h w)", i=2)
        block = own.enter_context(nc.Block())

        @block.sync
        def _(sp):
            def load(q, slot):
                sp.dma_start(x_in[slot][:], x_pairs[q]).then_inc(x_loaded[slot], 16)

            def store_z(q):
                sp.wait_ge(z_saved, NTOK * q + 2 * NTOK)
                after_wait(sp, sp_turn)
                sp.dma_start(d["z"][:, :, bass.ds(q * 128, 128)],
                             z_sb[:].rearrange("p c (a n) -> p (c a) n", n=128)).then_inc(z_stored, 16)

            def body(q, slot, use):
                if not is_first(q):
                    sp.wait_ge(xt_ready, NTOK * q)
                    after_wait(sp, sp_turn)
                    sp.wait_ge(r_done, NCONV * q)
                    after_wait(sp, sp_turn)
                if not (isinstance(q, int) and q == NPAIR - 1):
                    load(q + 1, 1 - slot)
                if not is_first(q):
                    store_z(q - 1)
                sp.wait_ge(x1_done, NTOK * q + NTOK)
                after_wait(sp, sp_turn)
                sp.dma_start(d["x1"][q], x1_t[:].rearrange("p c n -> p (c n)")).then_inc(x1_stored, 16)

            load(0, 0)
            two_by_two(sp, NPAIR, body)
            store_z(NPAIR - 1)
            sp.wait_ge(x1_stored, 16 * NPAIR)
            sp.wait_ge(z_stored, 16 * NPAIR)

        @block.tensor
        def _(pe):
            def step1(q):
                for c in range(NTOK):
                    if c == 0:
                        pe.wait_ge(sign_done, NCONV * q + 2 * NCONV)
                    elif c >= 2:
                        pe.wait_ge(z_saved, NTOK * q + NTOK + c - 1)
                    if c % 2 == 0:
                        pe.wait_ge(u_done, 4 * q + c // 2 + 1)
                    nc.tensor.matmul(p_cen[:, c % 2, :], keep["step1"][:, c // 2, :], u_t[:, c, :],
                                     start=True, stop=True).then_inc(z_ready, 1)

            def body(q, slot, use):
                x = x_in[slot]
                pe.wait_ge(x_loaded[slot], 16 * use)
                for c in range(NCONV):
                    if c < 2:
                        if not is_first(q) and c == 0:
                            pe.wait_ge(z_saved, NTOK * q)
                    else:
                        pe.wait_ge(sign_done, NCONV * q + c - 1)
                    nc.tensor.matmul(p_cen[:, c % 2, 0:CW], keep["center"][:], x[:, CW * c:CW * c + CW],
                                     start=True, stop=True).then_inc(cen_ready, 1)
                for c in range(NTOK):
                    if not (is_first(q) and c < 2):
                        pe.wait_ge(xt_copied, NTOK * q + c - 1)
                        pe.wait_ge(xt_squared, NTOK * q + c - 1)
                    for j in range(ACH):
                        a = ACH * c + j
                        mm = nc.tensor.matmul(p_xt[0:NB, c % 2, 128 * j:128 * j + 128], x[:, a:TOK:NA],
                                              keep["center"][:], start=True, stop=True)
                    mm.then_inc(xt_ready, 1)
                for c in range(NCONV):
                    pe.wait_ge(sign_done, NCONV * q + min(c + 2, NCONV))
                    if not (is_first(q) and c < 2):
                        pe.wait_ge(y_saved, NCONV * q + c - 1)
                    for t in range(9):
                        rows = slice(CROWS * c + t // 3, CROWS * c + t // 3 + CROWS)
                        mm = nc.tensor.matmul(p_conv[:, c % 2, 0:CW], keep["conv_w"][:, t, :],
                                              pad[:, rows, t % 3:t % 3 + WID], start=(t == 0), stop=(t == 8))
                    mm.then_inc(conv_ready, 1)
                if not is_first(q):
                    step1(q - 1)
                pe.wait_ge(r_done, NCONV * q + NCONV)
                for c in range(NTOK):
                    if not (is_first(q) and c < 2):
                        pe.wait_ge(x1_done, NTOK * q + c - 1)
                    for j in range(ACH):
                        a = ACH * c + j
                        mm = nc.tensor.transpose(p_rt[0:NB, c % 2, 128 * j:128 * j + 128], conv_y[:, a:TOK:NA],
                                                 keep["ident"][:])
                    mm.then_inc(rt_ready, 1)

            two_by_two(pe, NPAIR, body)
            for c in range(NTOK):
                q = NPAIR - 1
                pe.wait_ge(z_saved, NTOK * q + NTOK + max(c - 1, 0))
                if c % 2 == 0:
                    pe.wait_ge(u_done, 4 * q + c // 2 + 1)
                nc.tensor.matmul(p_cen[:, c % 2, :], keep["step1"][:, c // 2, :], u_t[:, c, :],
                                 start=True, stop=True).then_inc(z_ready, 1)

        @block.scalar
        def _(act):
            def save_z(q):
                if not is_first(q):
                    act.wait_ge(z_stored, 16 * q)
                for c in range(NTOK):
                    act.wait_ge(z_ready, NTOK * q + c + 1)
                    nc.scalar.activation(z_sb[:, c, :], p_cen[:, c % 2, :], ACT.Copy).then_inc(z_saved, 1)

            def body(q, slot, use):
                if not is_first(q):
                    act.wait_ge(conv_ready, NCONV * q)
                for c in range(NCONV):
                    act.wait_ge(cen_ready, NCONV * q + c + 1)
                    nc.scalar.activation(pad[:, 1 + CROWS * c:1 + CROWS * c + CROWS, 1:1 + WID],
                                         p_cen[:, c % 2, 0:CW].rearrange("p (h w) -> p h w", w=WID),
                                         ACT.Sign).then_inc(sign_done, 1)
                if not is_first(q):
                    act.wait_ge(x1_done, NTOK * q)
                for c in range(NTOK):
                    act.wait_ge(xt_ready, NTOK * q + c + 1)
                    nc.scalar.activation(xc_t[:, c, :], p_xt[0:NB, c % 2, :], ACT.Copy).then_inc(xt_copied, 1)
                    if not (is_first(q) and c < 2):
                        act.wait_ge(ssq1_done, NTOK * q + c - 1)
                    nc.scalar.activation(sq1[:, c % 2, :], p_xt[0:NB, c % 2, :], ACT.Square).then_inc(xt_squared, 1)
                if not is_first(q):
                    act.wait_ge(rt_ready, NTOK * q)
                for c in range(NCONV):
                    act.wait_ge(conv_ready, NCONV * q + c + 1)
                    nc.scalar.activation(conv_y[:, CW * c:CW * c + CW], p_conv[:, c % 2, 0:CW], ACT.Identity,
                                         bias=keep["bn"][:, 1:2], scale=keep["bn"][:, 0:1]).then_inc(y_saved, 1)
                if not is_first(q):
                    save_z(q - 1)

            act.sem_inc(z_saved, NTOK)
            two_by_two(act, NPAIR, body)
            save_z(NPAIR - 1)

        @block.gpsimd
        def _(pool):
            def normed(q):
                for c in range(4):
                    pool.wait_ge(rstd2_done, q + 1)
                    v = u_t[:, 2 * c:2 * c + 2, :].rearrange("p c (g n) -> p (c g) n", n=CH)
                    r = st2[:, 3, 16 * c:16 * c + 16].unsqueeze(2).to_broadcast([NB, 16, CH])
                    nc.gpsimd.tensor_tensor(v, v, r, ALU.mult).then_inc(u_done, 1)

            def body(q, slot, use):
                if not is_first(q):
                    normed(q - 1)
                for c in range(NCONV):
                    pool.wait_ge(y_saved, NCONV * q + c + 1)
                    v = conv_y[:, CW * c:CW * c + CW]
                    nc.gpsimd.tensor_tensor(v, v, x_in[slot][:, CW * c:CW * c + CW], ALU.add).then_inc(r_done, 1)
                for h in range(2):
                    pool.wait_ge(u_centered, 2 * q + h + 1)
                    v = u_t[:, 4 * h:4 * h + 4, :]
                    nc.gpsimd.tensor_tensor(sq2[:, 4 * h:4 * h + 4, :], v, v, ALU.mult).then_inc(sq2_done, 1)

            two_by_two(pool, NPAIR, body)
            normed(NPAIR - 1)

        @block.vector
        def _(dve):
            STEPS2 = 2 + 1 + RSQRT_STEPS
            STEPS1 = 1 + RSQRT_STEPS + 2 + 2 + 1
            STEPS = STEPS1 + STEPS2 - 1

            def rstd2(q, link):
                for h in range(2):
                    dve.wait_ge(sq2_done, 2 * q + h + 1)
                    link(nc.vector.tensor_reduce(st2[:, 1, 32 * h:32 * h + 32],
                                                 sq2[:, 4 * h:4 * h + 4, :].rearrange("p c (g n) -> p (c g) n", n=CH),
                                                 AX, ALU.add))
                link(nc.vector.tensor_scalar(st2[:, 2, :], st2[:, 1, :], 1.0 / CH, 1e-5, ALU.mult, ALU.add))
                if not is_first(q):
                    dve.wait_ge(u_done, 4 * q)
                rsqrt_steps(nc, link, st2[:, 3, :], st2[:, 2, :], st2[:, 4, :], st2[:, 5, :])

            def body(q, slot, use):
                first = is_first(q)
                base = 0 if first else STEPS1 + (q - 1) * (STEPS1 + 3 + RSQRT_STEPS)
                n = [0]

                def link(ins):
                    n[0] += 1
                    ins.then_inc(step, 1)
                    dve.wait_ge(step, base + n[0])

                for c in range(NTOK):
                    dve.wait_ge(xt_squared, NTOK * q + c + 1)
                    nc.vector.tensor_reduce(st1[:, 0, 8 * c:8 * c + 8],
                                            sq1[:, c % 2, :].rearrange("p (g n) -> p g n", n=CH),
                                            AX, ALU.add).then_inc(ssq1_done, 1)
                dve.wait_ge(ssq1_done, NTOK * q + NTOK)
                link(nc.vector.tensor_scalar(st1[:, 1, :], st1[:, 0, :], 1.0 / CH, 1e-6, ALU.mult, ALU.add))
                rsqrt_steps(nc, link, st1[:, 2, :], st1[:, 1, :], st1[:, 3, :], st1[:, 4, :])
                if not first:
                    rstd2(q - 1, link)
                    nc.vector.tensor_copy(st2[:, 4, 0:1], st2[:, 3, 0:1]).then_inc(rstd2_done, 1)
                dve.wait_ge(xt_copied, NTOK * q + NTOK)
                for h in range(2):
                    v = xc_t[:, 4 * h:4 * h + 4, :].rearrange("p c (g n) -> p (c g) n", n=CH)
                    link(nc.vector.tensor_tensor(v, v, st1[:, 2, 32 * h:32 * h + 32].unsqueeze(2)
                                                 .to_broadcast([NB, 32, CH]), ALU.mult))
                if not first:
                    dve.wait_ge(x1_stored, 16 * q)
                for c in range(NTOK):
                    dve.wait_ge(rt_ready, NTOK * q + c + 1)
                    nc.vector.tensor_tensor(x1_t[:, c, :], xc_t[:, c, :], p_rt[0:NB, c % 2, :],
                                            ALU.add).then_inc(x1_done, 1)
                for h in range(2):
                    dve.wait_ge(x1_done, NTOK * q + 4 * h + 4)
                    link(nc.vector.tensor_reduce(st2[:, 0, 32 * h:32 * h + 32],
                                                 x1_t[:, 4 * h:4 * h + 4, :].rearrange("p c (g n) -> p (c g) n", n=CH),
                                                 AX, ALU.add))
                link(nc.vector.tensor_scalar(st2[:, 0, :], st2[:, 0, :], 1.0 / CH, None, ALU.mult))
                if not first:
                    dve.wait_ge(z_ready, NTOK * q)
                for h in range(2):
                    shape = "p c (g n) -> p (c g) n"
                    nc.vector.tensor_tensor(
                        u_t[:, 4 * h:4 * h + 4, :].rearrange(shape, n=CH),
                        x1_t[:, 4 * h:4 * h + 4, :].rearrange(shape, n=CH),
                        st2[:, 0, 32 * h:32 * h + 32].unsqueeze(2).to_broadcast([NB, 32, CH]),
                        ALU.subtract).then_inc(u_centered, 1)
                assert n[0] == STEPS1 - 0 + (0 if first else 3 + RSQRT_STEPS), n[0]

            STEPS1 = 1 + RSQRT_STEPS + 2 + 3
            two_by_two(dve, NPAIR, body)
            n = [STEPS1 + (NPAIR - 1) * (STEPS1 + 3 + RSQRT_STEPS)]

            def link(ins):
                n[0] += 1
                ins.then_inc(step, 1)
                dve.wait_ge(step, n[0])
            rstd2(NPAIR - 1, link)
            nc.vector.tensor_copy(st2[:, 4, 0:1], st2[:, 3, 0:1]).then_inc(rstd2_done, 1)


PLAN = [("x", 4), ("h", 4), ("t1", 4), ("h", 4), ("t2", 4), ("h", 8), ("inv", 4), ("mix", 4)]
TAIL = ("t1", "t2", "inv")
RING = 6


def unit_chunks():
    seen, out = {}, []
    for stage, count in PLAN:
        for _ in range(count):
            k = seen.get(stage, 0)
            seen[stage] = k + 1
            out.append((stage, k, len(out)))
    return out


def chunk_is_there(stage, u):
    return (u > 0) if stage in TAIL else (u < NUNIT)


def chunks_until(u, p, engine=None):
    plan = unit_chunks()
    if isinstance(u, int):
        return sum(1 for w in range(u + 1) for stage, _, at in plan
                   if chunk_is_there(stage, w) and (w < u or at <= p) and engine in (None, at % 2))
    per_unit = sum(1 for _, _, at in plan if engine in (None, at % 2))
    missing = sum(1 for stage, _, at in plan if stage in TAIL and engine in (None, at % 2))
    return per_unit * u - missing + sum(1 for _, _, at in plan if at <= p and engine in (None, at % 2))


def mix_frequencies(nc, d, keep):
    chunks = unit_chunks()
    NCH = len(chunks)
    assert NCH % RING == 0 and NCH % 2 == 0 and RING % 2 == 0
    pos = {(s, k): p for s, k, p in chunks}
    with ExitStack() as own:
        def sb(name, shape, dt=F32):
            return own.enter_context(nc.sbuf_tensor(name, shape, dt))

        def sem(name):
            return own.enter_context(nc.semaphore(name))

        z_in = [sb(f"z_in{i}", [128, ZCOLS]) for i in range(2)]
        fwd = [sb(f"fwd{i}", [128, 3, 128]) for i in range(2)]
        inv = [sb(f"inv{i}", [128, 4, 128]) for i in range(2)]
        xf = sb("xf", [128, NF, NIMG])
        hf = sb("hf", [128, NF, 2, CH])
        y1 = sb("y1", [128, 16, 128])
        y2 = sb("y2", [128, 16, 2, NF])
        yt = sb("yt", [128, 2, 16, CH])
        wf = sb("wf", [128, 2, 16, CH])
        vmov = keep["vmov"]
        ring = own.enter_context(nc.psum_tensor("ring", [128, RING, 512], F32))
        p_v = own.enter_context(nc.psum_tensor("p_v", [128, 512], F32))

        z_loaded = [sem(f"z_loaded{i}") for i in range(2)]
        inv_loaded = [sem(f"inv_loaded{i}") for i in range(2)]
        chunk_ready, v_ready, v_saved, w_stored, w_free = (
            sem(n) for n in ("chunk_ready", "v_ready", "v_saved", "w_stored", "w_free"))
        sp_turn, pool_turn = sem("sp_turn"), sem("pool_turn")
        saved = [sem("saved_by_act"), sem("saved_by_dve")]

        z_units = d["z"].rearrange("(u r) a c -> u (r a) c", r=4)
        w_units = d["w"].rearrange("(u s r) a (h m) e -> u s h a r (m e)", s=2, r=2, h=2)
        block = own.enter_context(nc.Block())

        def out_of(stage, k, u_prev):
            def view(bank):
                if stage == "x":
                    return (xf[:, :, 8 * k:8 * k + 8].rearrange("p f i -> p i f"),
                            bank.rearrange("p (i f) -> p i f", f=NF))
                if stage == "h":
                    return (hf[:, :, :, 4 * k:4 * k + 4].rearrange("p f r e -> p e r f"),
                            bank.rearrange("p (e r f) -> p e r f", r=2, f=NF))
                if stage == "mix":
                    return y1[:, 4 * k:4 * k + 4, :].rearrange("p f n -> p (f n)"), bank
                if stage == "t1":
                    return (y2[:, :, :, 16 * k:16 * k + 16].rearrange("p m h f -> p f h m"),
                            bank.rearrange("p (f h m) -> p f h m", h=2, m=16))
                if stage == "t2":
                    return (yt[:, :, 4 * k:4 * k + 4, :].rearrange("p r m e -> p m r e"),
                            bank.rearrange("p (m r e) -> p m r e", r=2, e=CH))
                r, g = divmod(k, 2)
                return wf[:, r, 8 * g:8 * g + 8, :].rearrange("p m e -> p (m e)"), bank
            return view

        @block.sync
        def _(sp):
            def load(u, slot):
                sp.dma_start(z_in[slot][:], z_units[u]).then_inc(z_loaded[slot], 16)
                sp.dma_start(fwd[slot][:].rearrange("p n f -> p (n f)"), d["c_fwd"][u]).then_inc(z_loaded[slot], 16)

            def load_inv(u, slot):
                sp.dma_start(inv[slot][:].rearrange("p n f -> p (n f)"), d["c_inv"][u]).then_inc(inv_loaded[slot], 16)

            def body(u, slot, use):
                if not (isinstance(u, int) and u == NUNIT - 1):
                    if not is_first(u):
                        sp.wait_ge(chunk_ready, chunks_until(u - 1, pos["mix", 3]))
                        after_wait(sp, sp_turn)
                    load(u + 1, 1 - slot)
                    if not is_first(u):
                        sp.wait_ge(chunk_ready, chunks_until(u, pos["inv", 3]))
                        after_wait(sp, sp_turn)
                    load_inv(u + 1, 1 - slot)

            load(0, 0)
            load_inv(0, 0)
            two_by_two(sp, NUNIT, body)

        @block.gpsimd
        def _(pool):
            def store(u):
                for e in range(2):
                    pool.wait_ge(saved[e], chunks_until(u + 1, pos["inv", 3], e))
                after_wait(pool, pool_turn)
                for h in range(2):
                    for s in range(2):
                        rows = slice(64 * h + 32 * s, 64 * h + 32 * s + 32)
                        nc.gpsimd.dma_start(w_units[u, s, h], wf[rows].rearrange("p r m e -> p r (m e)")).then_inc(w_stored, 16)
                pool.wait_ge(w_stored, 64 * (u + 1))
                pool.sem_inc(w_free, 1)

            pool.sem_inc(w_free, 1)
            store(0)
            with pool.Fori(1, NUNIT - 1) as u:
                store(u)
            store(NUNIT - 1)

        def bank_free(eng, u, p):
            if not isinstance(u, int):
                eng.wait_ge(saved[p % 2], chunks_until(u, p, p % 2) - RING // 2)
                return
            before = [(w, at) for w in range(u + 1) for stage, _, at in chunks
                      if chunk_is_there(stage, w) and at % RING == p % RING and (w < u or at < p)]
            if before:
                eng.wait_ge(saved[p % 2], chunks_until(*before[-1], p % 2))

        def all_saved(eng, u, p):
            for e in range(2):
                eng.wait_ge(saved[e], chunks_until(u, p, e))

        @block.tensor
        def _(pe):
            def unit(u, slot, use, head, tail):
                if head:
                    pe.wait_ge(z_loaded[slot], 32 * use)
                    if not is_first(u):
                        pe.wait_ge(v_saved, u)
                    lhs = z_in[slot][:, NIMG * CH:ZCOLS]
                    nc.tensor.matmul(p_v[0:NK, 0:128], lhs, fwd[slot][:, 1, :], start=True, stop=True)
                    nc.tensor.matmul(p_v[KI:KROWS, 0:128], lhs, fwd[slot][:, 2, :], start=True,
                                     stop=True).then_inc(v_ready, 1)
                for stage, k, p in chunks:
                    if not (tail if stage in TAIL else head):
                        continue
                    bank_free(pe, u, p)
                    bank = ring[:, p % RING, :]
                    if stage == "x":
                        for i in range(8):
                            z = z_in[slot][:, CH * (8 * k + i):CH * (8 * k + i) + CH]
                            for r in range(2):
                                mm = nc.tensor.matmul(bank[CH * r:CH * r + CH, NF * i:NF * i + NF], z,
                                                      fwd[slot][:, 0, NF * r:NF * r + NF], start=True, stop=True)
                    elif stage == "h":
                        if k == 0:
                            pe.wait_ge(v_saved, u + 1)
                        for i in range(4):
                            mm = nc.tensor.matmul(bank[:, 128 * i:128 * i + 128], keep["mt"][:, 4 * k + i, :],
                                                  vmov[:], start=True, stop=True)
                    elif stage == "mix":
                        if k == 0:
                            all_saved(pe, u, pos["h", 15])
                        for i in range(4):
                            for j in range(4):
                                f = 16 * k + 4 * i + j
                                mm = nc.tensor.matmul(bank[32 * j:32 * j + 32, 128 * i:128 * i + 128], xf[:, f, :],
                                                      hf[:, f, :, :].rearrange("p r e -> p (r e)"),
                                                      start=True, stop=True, tile_position=(0, 32 * j))
                    elif stage == "t1":
                        if k == 0:
                            all_saved(pe, u - 1, pos["mix", 3])
                        for i in range(4):
                            mm = nc.tensor.transpose(bank[:, 128 * i:128 * i + 128], y1[:, 4 * k + i, :], keep["ident"][:])
                    elif stage == "t2":
                        if k == 0:
                            all_saved(pe, u, pos["t1", 3])
                        for i in range(4):
                            mm = nc.tensor.transpose(bank[:, 128 * i:128 * i + 128],
                                                     y2[:, 4 * k + i, :, :].rearrange("p h f -> p (h f)"), keep["ident"][:])
                    else:
                        if k == 0:
                            all_saved(pe, u, pos["t2", 3])
                            pe.wait_ge(inv_loaded[1 - slot], 16 * (use if slot else use - 1))
                        r_out, g = divmod(k, 2)
                        for r in range(2):
                            mm = nc.tensor.matmul(bank, inv[1 - slot][:, 2 * r + r_out, :],
                                                  yt[:, r, 8 * g:8 * g + 8, :].rearrange("p m e -> p (m e)"),
                                                  start=(r == 0), stop=(r == 1))
                    mm.then_inc(chunk_ready, 1)

            def body(u, slot, use):
                unit(u, slot, use, True, not is_first(u))

            two_by_two(pe, NUNIT, body)
            unit(NUNIT, 0, NUNIT // 2 + 1, False, True)

        def saver(eng, which, copy):
            def unit(u, head, tail):
                if head and which:
                    eng.wait_ge(v_ready, u + 1)
                    copy(vmov[0:NK, :], p_v[0:NK, 0:128])
                    copy(vmov[KI:KROWS, :], p_v[KI:KROWS, 0:128]).then_inc(v_saved, 1)
                for stage, k, p in chunks:
                    if p % 2 != which or not (tail if stage in TAIL else head):
                        continue
                    eng.wait_ge(chunk_ready, chunks_until(u, p))
                    if stage == "inv" and k < 2:
                        eng.wait_ge(w_free, u)
                    dst, src = out_of(stage, k, u)(ring[:, p % RING, :])
                    copy(dst, src).then_inc(saved[which], 1)

            two_by_two(eng, NUNIT, lambda u, slot, use: unit(u, True, not is_first(u)))
            unit(NUNIT, False, True)

        @block.scalar
        def _(act):
            saver(act, 0, lambda dst, src: nc.scalar.activation(dst, src, ACT.Copy))

        @block.vector
        def _(dve):
            saver(dve, 1, lambda dst, src: nc.vector.tensor_copy(dst, src))


def finish(nc, d, keep):
    with ExitStack() as own:
        def sb(name, shape, dt=F32):
            return own.enter_context(nc.sbuf_tensor(name, shape, dt))

        def sem(name):
            return own.enter_context(nc.semaphore(name))

        w_in = [sb(f"w_in{i}", [NROW, NA, 128]) for i in range(2)]
        x1_in = [sb(f"x1_in{i}", [NB, NA, 128]) for i in range(2)]
        out_sb = [sb(f"out_sb{i}", [128, NB, NA]) for i in range(2)]
        p_out = own.enter_context(nc.psum_tensor("p_out", [128, 8, 512], F32))
        w_loaded = [sem(f"w_loaded{i}") for i in range(2)]
        out_stored = [sem(f"out_stored{i}") for i in range(2)]
        out_ready = sem("out_ready")
        sp_turn, pool_turn = sem("sp_turn"), sem("pool_turn")
        saved = [sem("out_by_act"), sem("out_by_dve")]
        w_rows = d["w"].rearrange("r a i e -> r a (i e)")
        out_pairs = d["out"].rearrange("(q i) c h w -> q (i c) (h w)", i=2)
        block = own.enter_context(nc.Block())

        @block.sync
        def _(sp):
            def load(q, slot):
                sp.dma_start(w_in[slot][:], w_rows[:, :, bass.ds(q * 128, 128)]).then_inc(w_loaded[slot], 16)
                sp.dma_start(x1_in[slot][:].rearrange("p a n -> p (a n)"), d["x1"][q]).then_inc(w_loaded[slot], 16)

            def body(q, slot, use):
                if not (isinstance(q, int) and q == NPAIR - 1):
                    if not is_first(q):
                        sp.wait_ge(out_ready, NTOK * q)
                        after_wait(sp, sp_turn)
                    load(q + 1, 1 - slot)

            load(0, 0)
            two_by_two(sp, NPAIR, body)

        @block.gpsimd
        def _(pool):
            def body(q, slot, use):
                for e in range(2):
                    pool.wait_ge(saved[e], 4 * q + 4)
                after_wait(pool, pool_turn)
                nc.gpsimd.dma_start(out_pairs[q], out_sb[slot][:].rearrange("p b a -> p (b a)")).then_inc(out_stored[slot], 16)

            two_by_two(pool, NPAIR, body)
            for s in range(2):
                pool.wait_ge(out_stored[s], 16 * (NPAIR // 2))

        @block.tensor
        def _(pe):
            def body(q, slot, use):
                pe.wait_ge(w_loaded[slot], 32 * use)
                for c in range(NTOK):
                    if not is_first(q):
                        pe.wait_ge(saved[c % 2], 4 * q - 4 + c // 2 + 1)
                    for j in range(ACH):
                        a = ACH * c + j
                        to = p_out[:, c, NB * j:NB * j + NB]
                        nc.tensor.matmul(to, w_in[slot][:, a, :], keep["last"][:, a // MASKG, :], start=True, stop=False)
                        mm = nc.tensor.matmul(to, x1_in[slot][:, a, :], keep["ident"][0:NB, 0:NB], start=False, stop=True)
                    mm.then_inc(out_ready, 1)

            two_by_two(pe, NPAIR, body)

        def saver(eng, which, copy):
            def body(q, slot, use):
                if not (isinstance(q, int) and q < 2):
                    eng.wait_ge(out_stored[slot], 16 * (use - 1))
                for c in range(which, NTOK, 2):
                    eng.wait_ge(out_ready, NTOK * q + c + 1)
                    copy(out_sb[slot][:, :, ACH * c:ACH * c + ACH].rearrange("p b a -> p a b"),
                         p_out[:, c, 0:ACH * NB].rearrange("p (a b) -> p a b", b=NB)).then_inc(saved[which], 1)

            body(0, 0, 1)
            body(1, 1, 1)
            with eng.Fori(1, NPAIR // 2) as h:
                body(2 * h, 0, h + 1)
                body(2 * h + 1, 1, h + 1)

        @block.scalar
        def _(act):
            saver(act, 0, lambda dst, src: nc.scalar.activation(dst, src, ACT.Copy))

        @block.vector
        def _(dve):
            saver(dve, 1, lambda dst, src: nc.vector.tensor_copy(dst, src))


def build(nc, d):
    d["z"] = nc.dram_tensor("z_scratch", [NROW, NA, ZCOLS], F32).ap()
    d["w"] = nc.dram_tensor("w_scratch", [NROW, NA, NIMG, CH], F32).ap()
    d["x1"] = nc.dram_tensor("x1_scratch", [NPAIR, NB, NA * 128], F32).ap()
    with ExitStack() as ctx:
        def sb(name, shape, dt=F32):
            return ctx.enter_context(nc.sbuf_tensor(name, shape, dt))

        keep = {
            "ident": sb("ident", [128, 128]),
            "center": sb("center", [128, 128]),
            "bn": sb("bn_scale_bias", [128, 2]),
            "conv_w": sb("conv_w", [128, 9, 128], BF16),
            "step1": sb("step1_masked", [NB, NMASK, NROW]),
            "last": sb("last_masked", [NROW, NMASK, NB]),
            "mt": sb("mix_stationary", [KROWS, CH, 128]),
            "vmov": sb("filters_moving", [KROWS, 128]),
            "pad": sb("signs_padded", [128, HGT + 2, WID + 2], BF16),
        }
        prepare(nc, ctx, d, keep)
        norm_and_convolve(nc, d, keep)
        mix_frequencies(nc, d, keep)
        finish(nc, d, keep)


_INS = {
    "x": "x", "L0_conv_weight": "weight", "L0_conv_gamma": "gamma", "L0_conv_beta": "beta",
    "L0_conv_bn_mean": "bn_mean", "L0_conv_bn_var": "bn_var", "L0_ffn_sigma": "sigma", "L0_ffn_phi": "phi",
    "L0_ffn_M_u": "M_u", "L0_ffn_M_phi_plus": "M_plus", "L0_ffn_M_phi_minus": "M_minus",
    "L0_ffn_log_weights": "log_weights", "L0_ffn_gumbel": "gumbel",
}


def kernel(**inputs):
    import concourse.bacc as _bacc
    from concourse.bass_utils import run_bass_kernel_spmd as _run

    nc = _bacc.Bacc("TRN2", target_bir_lowering=False, num_devices=1)
    arrays, d = {}, {}
    given = {short: np.ascontiguousarray(inputs[name]) for name, short in _INS.items()}
    for name, a in {**given, **constants()}.items():
        arrays["in_" + name] = a
        d[name] = nc.dram_tensor("in_" + name, a.shape, mybir.dt.from_np(a.dtype), kind="ExternalInput").ap()
    d["out"] = nc.dram_tensor("out_dram", given["x"].shape, F32, kind="ExternalOutput").ap()
    build(nc, d)
    r = _run(nc, [arrays], core_ids=[0])
    return r.results[0]["out_dram"]
```

```python
from contextlib import ExitStack

import numpy as np

import concourse.bass as bass
from concourse import mybir

F32 = mybir.dt.float32
BF16 = mybir.dt.bfloat16
F16 = mybir.dt.float16
I32 = mybir.dt.int32
ALU = mybir.AluOpType
ACT = mybir.ActivationFunctionType
AX = mybir.AxisListType.X

NIMG, CH, HGT, WID = 32, 64, 56, 56
TOK = HGT * WID
NBR = 4
KF, KU = 16, 3
PHI_LEN = 2048
NFFT = 4096

NA = 32
NB = TOK // NA
NSLOT = 64
NALPHA = 32
NROW = 2 * NSLOT
NUNIT = NSLOT // 2
NF = 2 * NALPHA
NK = 2 * KF + KU
KI = 64
KROWS = KI + NK
NPAIR = NIMG // 2
ZCOLS = NIMG * CH + NK

CROWS = 8
NCONV = HGT // CROWS
CW = CROWS * WID
ACH = 4
NTOK = NA // ACH
TW = ACH * 2 * CH
MASKG = 8
NMASK = NA // MASKG

ROWS_A = (NBR - 1) * NK
ROWS_B = NK
HALF_TOP = 14
EXPONENT = 0x7F800000
RSQRT_MAGIC = 0x5F3759DF
NEWTON = 3


def slot_frequencies(s):
    if s:
        return [s + 128 * al for al in range(NALPHA)]
    return [128 * al for al in range(16)] + [64 + 128 * al for al in range(16)]


def constants():
    b = np.arange(NB)
    s1 = np.zeros((NB, NROW))
    s2 = np.zeros((NROW, NB))
    s1[:, 0], s1[:, 1] = 1.0, (-1.0) ** b
    s2[0], s2[1] = 1.0, (-1.0) ** b
    for s in range(1, NSLOT):
        th = 2 * np.pi * s * b / 128
        s1[:, 2 * s], s1[:, 2 * s + 1] = np.cos(th), -np.sin(th)
        s2[2 * s], s2[2 * s + 1] = np.cos(th), -np.sin(th)

    a = np.arange(NA)[:, None]
    fwd = np.zeros((NUNIT, 2, 2, NA, 2, 2, NALPHA))
    inv = np.zeros((NUNIT, 2, 2, 2, NALPHA, NA))
    for s in range(NSLOT):
        u, sl = divmod(s, 2)
        f = np.array(slot_frequencies(s))[None, :]
        th = 2 * np.pi * f * a / NFFT
        c, sn = np.cos(th), np.sin(th)
        re_re, re_im, im_re, im_im = c.copy(), -sn, sn.copy(), c.copy()
        ci, si = 2 * c.T / NFFT, 2 * sn.T / NFFT
        g = np.array([[ci, si], [-si, ci]])
        if s == 0:
            z = np.zeros((NA, 16))
            re_re = np.hstack([c[:, :16], z])
            re_im = np.hstack([-sn[:, :16], z])
            im_re = np.hstack([z, c[:, 16:]])
            im_im = np.hstack([z, -sn[:, 16:]])
            re_im[:, 0] = (-1.0) ** a[:, 0]
            g[:] = 0.0
            g[0, 0, :16], g[1, 0, :16] = ci[:16], -si[:16]
            g[0, 1, 16:], g[1, 1, 16:] = ci[16:], -si[16:]
            g[0, 0, 0] = 1.0 / NFFT
            g[1, 0, 0] = (-1.0) ** a[:, 0] / NFFT
        x = np.array([[re_re, re_im], [im_re, im_im]])
        fwd[u, sl, :, :, :, sl] = x.transpose(0, 2, 1, 3)
        inv[u, sl] = g
    fwd = fwd.reshape(NUNIT, 128, 128)
    ib = np.zeros((NUNIT, 2, 2, NALPHA, 2, 2, 2, NA))
    for h in range(2):
        ib[:, h, :, :, :, h] = inv.transpose(0, 2, 4, 1, 3, 5)
    inv = ib.reshape(NUNIT, 128, 2 * 128)

    center = np.kron(np.eye(2), np.eye(CH) - 1.0 / CH)
    t = (np.arange(NMASK) * MASKG)[None, :] + NA * b[:, None]
    mask = np.stack([t < (TOK >> i) for i in range(NBR)], -1)
    mask_col = mask.reshape(NB, NMASK * NBR)
    mask_row = np.broadcast_to(mask.transpose(1, 2, 0).reshape(1, -1), (128, NMASK * NBR * NB))
    sign_a = np.broadcast_to((-1.0) ** np.arange(NA), (KI, NA))
    eye = np.tile(np.eye(NK), (NBR, 1))
    select = np.zeros((NBR * NK, KROWS))
    select[:, 0:NK], select[:, KI:KROWS] = eye, -eye
    branch = np.repeat(np.eye(NBR), NK, 0)
    out = {
        "c_select": select, "c_branch": branch,
        "c_step1": s1, "c_step_last": s2, "c_fwd": fwd, "c_inv": inv, "c_center": center,
        "c_ident": np.eye(128), "c_mask_col": mask_col, "c_mask_row": mask_row, "c_sign_a": sign_a,
    }
    return {k: np.ascontiguousarray(v, dtype=np.float32) for k, v in out.items()}


def rsqrt_steps(nc, link, y, v, t0, t1):
    link(nc.vector.tensor_scalar(t0.bitcast(I32), v.bitcast(I32), 1, None, ALU.logical_shift_right))
    link(nc.vector.tensor_scalar(y.bitcast(I32), t0.bitcast(I32), -1.0, float(RSQRT_MAGIC), ALU.mult, ALU.add))
    for _ in range(NEWTON):
        link(nc.vector.tensor_tensor(t0, y, y, ALU.mult))
        link(nc.vector.scalar_tensor_tensor(t1, t0, -0.5, v, ALU.mult, ALU.mult))
        link(nc.vector.scalar_tensor_tensor(y, t1, 1.5, y, ALU.add, ALU.mult))


RSQRT_STEPS = 2 + 3 * NEWTON


def two_by_two(eng, count, body, last_apart=0):
    body(0, 0, 1)
    body(1, 1, 1)
    with eng.Fori(1, (count - last_apart) // 2) as h:
        body(2 * h, 0, h + 1)
        body(2 * h + 1, 1, h + 1)
    for n in range(count - last_apart, count):
        body(n, n % 2, n // 2 + 1)


def known(n, *values):
    return isinstance(n, int) and n in values


def after_wait(eng, sem):
    eng.sem_inc(sem, 1)


def is_first(n):
    return known(n, 0)


def prepare(nc, d, keep):
    with ExitStack() as own:
        def sb(name, shape, dt=F32):
            return own.enter_context(nc.sbuf_tensor(name, shape, dt))

        def sem(name):
            return own.enter_context(nc.semaphore(name))

        w_raw = sb("w_raw", [128, CH * 9])
        w_diag = sb("w_diag", [128, 9, 128])
        bn = sb("bn", [128, 16])
        mix = sb("mix", [128, 64])
        s1 = sb("s1", [NB, NROW])
        s2 = sb("s2", [NROW, NB])
        mask_col = sb("mask_col", [NB, NMASK * NBR])
        mask_row = sb("mask_row", [128, NMASK, NBR, NB])
        mask_cs = sb("mask_cs", [NB, NMASK])
        mask_rs = sb("mask_rs", [128, NMASK, NB])
        sgn_a = sb("sgn_a", [KI, NA])
        phi = sb("phi", [KI, NA, KF])
        sig = sb("sig", [KI, 3, KF])
        filt = sb("filt", [KI, NA, NK])
        filt_z = sb("filt_z", [NROW, NA, NK])
        select = [sb("select_a", [ROWS_A, KROWS]), sb("select_b", [ROWS_B, KROWS])]
        branch = [sb("branch_a", [ROWS_A, NBR]), sb("branch_b", [ROWS_B, NBR])]
        p_w = own.enter_context(nc.psum_tensor("p_w", [128, 4, 512], F32))
        p_f = own.enter_context(nc.psum_tensor("p_f", [128, 4, 512], F32))

        loaded = {n: sem("loaded_" + n) for n in ("conv", "bn", "mix", "mask", "phi", "const", "sel")}
        zeroed, signed, turned = sem("zeroed"), sem("signed"), sem("turned")
        pow_done, exp_in, exp_done = sem("pow_done"), sem("exp_in"), sem("exp_done")
        step, filt_ready, filt_dft, filt_saved, filt_stored = (
            sem(n) for n in ("prep_step", "filt_ready", "filt_dft", "filt_saved", "filt_stored"))

        block = own.enter_context(nc.Block())

        @block.sync
        def _(sp):
            for h in range(2):
                half = slice(CH * h, CH * h + CH)
                sp.dma_start(w_raw[half, :], d["weight"].rearrange("o i h w -> o (i h w)")).then_inc(loaded["conv"], 16)
                for n, name in enumerate(("gamma", "beta", "bn_mean", "bn_var")):
                    sp.dma_start(bn[half, n:n + 1], d[name].rearrange("(o a) -> o a", a=1)).then_inc(loaded["bn"], 16)
            sp.dma_start(keep["ident"][:], d["c_ident"]).then_inc(loaded["const"], 16)
            sp.dma_start(keep["center"][:], d["c_center"]).then_inc(loaded["const"], 16)
            sp.dma_start(phi[:], d["phi"].rearrange("(b a) k -> b a k", a=NA)).then_inc(loaded["phi"], 16)
            sp.dma_start(sig[:, 0, :], d["sigma"].partition_broadcast(KI)).then_inc(loaded["phi"], 16)
            sp.dma_start(sgn_a[:], d["c_sign_a"]).then_inc(loaded["phi"], 16)
            sp.dma_start(mix[:, 0:4], d["log_weights"].partition_broadcast(128)).then_inc(loaded["mix"], 16)
            sp.dma_start(mix[:, 4:8], d["gumbel"].partition_broadcast(128)).then_inc(loaded["mix"], 16)
            sp.dma_start(s1[:], d["c_step1"]).then_inc(loaded["mask"], 16)
            sp.dma_start(s2[:], d["c_step_last"]).then_inc(loaded["mask"], 16)
            sp.dma_start(mask_col[:], d["c_mask_col"]).then_inc(loaded["mask"], 16)
            sp.dma_start(mask_row[:].rearrange("p g i b -> p (g i b)"), d["c_mask_row"]).then_inc(loaded["mask"], 16)
            sp.dma_start(select[0][:], d["c_select"][0:ROWS_A, :]).then_inc(loaded["sel"], 16)
            sp.dma_start(select[1][:], d["c_select"][ROWS_A:ROWS_A + ROWS_B, :]).then_inc(loaded["sel"], 16)
            sp.dma_start(branch[0][:], d["c_branch"][0:ROWS_A, :]).then_inc(loaded["sel"], 16)
            sp.dma_start(branch[1][:], d["c_branch"][ROWS_A:ROWS_A + ROWS_B, :]).then_inc(loaded["sel"], 16)
            x_pairs = d["x"].rearrange("(q i) c h w -> q (i c) (h w)", i=2)
            for q in range(2):
                sp.dma_start(keep["x_in"][q][:], x_pairs[q]).then_inc(keep["x_loaded"][q], 16)
            for i in range(NBR):
                tile, base = (keep["m_raw"][0], i * NK) if i < NBR - 1 else (keep["m_raw"][1], 0)
                for row, n, src in ((0, KF, d["M_plus"]), (KF, KF, d["M_minus"]), (2 * KF, KU, d["M_u"])):
                    sp.dma_start(tile[base + row:base + row + n, :],
                                 src[i].rearrange("k d e -> k (d e)")).then_inc(keep["m_loaded"], 16)
            sp.wait_ge(filt_saved, 4)
            sp.dma_start(d["z"][:, :, NIMG * CH:ZCOLS], filt_z[:]).then_inc(filt_stored, 16)
            sp.wait_ge(filt_stored, 16)

        @block.gpsimd
        def _(pool):
            nc.gpsimd.memset(sig[:, 1, :], 0.25).then_inc(zeroed, 1)
            pool.wait_ge(zeroed, 1)
            pool.wait_ge(loaded["phi"], 48)
            nc.gpsimd.tensor_tensor(sig[:, 2, :], sig[:, 0, :], sig[:, 1, :], ALU.pow).then_inc(pow_done, 1)
            nc.gpsimd.memset(keep["pad"][:], 0.0)
            nc.gpsimd.memset(keep["peaks"][:], 0.0).then_inc(zeroed, 1)

        @block.scalar
        def _(act):
            act.wait_ge(loaded["conv"], 32)
            act.wait_ge(step, 1)
            for h in range(2):
                half = slice(CH * h, CH * h + CH)
                nc.scalar.activation(w_diag[half, :, half], w_raw[half, :].rearrange("o (i t) -> o t i", t=9),
                                     ACT.Sign).then_inc(signed, 1)
            act.wait_ge(exp_in, 1)
            nc.scalar.activation(mix[:, 12:16], mix[:, 12:16], ACT.Exp).then_inc(exp_done, 1)

        @block.tensor
        def _(pe):
            pe.wait_ge(loaded["const"], 32)
            pe.wait_ge(signed, 2)
            for t in range(9):
                mm = nc.tensor.transpose(p_w[:, t // 4, 128 * (t % 4):128 * (t % 4) + 128], w_diag[:, t, :],
                                         keep["ident"][:])
            mm.then_inc(turned, 1)
            pe.wait_ge(filt_ready, 1)
            for c in range(4):
                nc.tensor.matmul(p_f[:, c, 0:8 * NK], s1[0:KI, :], filt[:, 8 * c:8 * c + 8, :],
                                 start=True, stop=True).then_inc(filt_dft, 1)

        @block.vector
        def _(dve):
            n = [0]

            def link(ins):
                n[0] += 1
                ins.then_inc(step, 1)
                dve.wait_ge(step, n[0])

            link(nc.vector.memset(w_diag[:], 0.0))
            link(nc.vector.memset(filt[:], 0.0))
            for k in range(KU):
                link(nc.vector.memset(filt[0:1, k, 2 * KF + k:2 * KF + k + 1], 1.0))
            dve.wait_ge(pow_done, 1)
            link(nc.vector.tensor_tensor(filt[:, :, 0:KF], phi[:], sig[:, 2:3, :].to_broadcast([KI, NA, KF]), ALU.mult))
            link(nc.vector.tensor_tensor(filt[:, :, KF:2 * KF], filt[:, :, 0:KF],
                                         sgn_a[:].unsqueeze(2).to_broadcast([KI, NA, KF]), ALU.mult))
            dve.wait_ge(zeroed, 2)
            link(nc.vector.tensor_reduce(keep["peaks"][0:KI, 2:3], filt[:, :, 0:KF], mybir.AxisListType.XY,
                                         ALU.max, apply_absolute_value=True))
            dve.wait_ge(loaded["mask"], 64)
            nc.vector.memset(bn[:, 15:16], 0.0).then_inc(filt_ready, 1)

            dve.wait_ge(loaded["bn"], 128)
            dve.wait_ge(loaded["conv"], 32)
            link(nc.vector.tensor_reduce(bn[:, 4:5], w_raw[:], AX, ALU.add, apply_absolute_value=True))
            link(nc.vector.tensor_scalar(bn[:, 5:6], bn[:, 3:4], 1e-5, None, ALU.add))
            rsqrt_steps(nc, link, bn[:, 6:7], bn[:, 5:6], bn[:, 7:8], bn[:, 8:9])
            link(nc.vector.tensor_tensor(bn[:, 9:10], bn[:, 6:7], bn[:, 0:1], ALU.mult))
            link(nc.vector.scalar_tensor_tensor(keep["bn"][:, 0:1], bn[:, 4:5], 1.0 / (9 * CH), bn[:, 9:10],
                                                ALU.mult, ALU.mult))
            link(nc.vector.tensor_tensor(bn[:, 10:11], bn[:, 2:3], bn[:, 9:10], ALU.mult))
            link(nc.vector.tensor_tensor(keep["bn"][:, 1:2], bn[:, 1:2], bn[:, 10:11], ALU.subtract))
            dve.wait_ge(turned, 1)
            link(nc.vector.tensor_copy(keep["conv_w"][:].rearrange("p t o -> p (t o)"),
                                       p_w[:, 0:3, :].rearrange("p a b -> p (a b)")[:, 0:9 * 128]))

            dve.wait_ge(loaded["mix"], 32)
            link(nc.vector.tensor_tensor(mix[:, 8:12], mix[:, 0:4], mix[:, 4:8], ALU.add))
            link(nc.vector.tensor_reduce(mix[:, 16:17], mix[:, 8:12], AX, ALU.max))
            nc.vector.tensor_scalar(mix[:, 12:16], mix[:, 8:12], mix[:, 16:17], None, ALU.subtract).then_inc(exp_in, 1)
            dve.wait_ge(exp_done, 1)
            link(nc.vector.tensor_reduce(mix[:, 17:18], mix[:, 12:16], AX, ALU.add))
            link(nc.vector.reciprocal(mix[:, 18:19], mix[:, 17:18]))
            link(nc.vector.tensor_scalar(mix[:, 20:24], mix[:, 12:16], mix[:, 18:19], None, ALU.mult))
            link(nc.vector.tensor_reduce(mix[:, 19:20], mix[:, 20:24], AX, ALU.max))
            link(nc.vector.tensor_scalar(mix[:, 24:28], mix[:, 20:24], mix[:, 19:20], None, ALU.is_ge))
            link(nc.vector.tensor_scalar(mix[:, 28:32], mix[:, 24:28], -1.0, 1.0, ALU.mult, ALU.add))
            hard, soft, weight = mix[:, 32:36], mix[:, 20:24], mix[:, 36:40]
            link(nc.vector.tensor_copy(mix[:, 32:36], mix[:, 24:28]))
            for i in range(1, NBR):
                for j in range(i):
                    link(nc.vector.tensor_tensor(mix[:, 32 + i:33 + i], mix[:, 32 + i:33 + i], mix[:, 28 + j:29 + j],
                                                 ALU.mult))
            link(nc.vector.tensor_tensor(mix[:, 40:44], hard, soft, ALU.subtract))
            link(nc.vector.tensor_tensor(weight, mix[:, 40:44], soft, ALU.add))

            for i in range(NBR):
                mc = mask_col[:].rearrange("b (g i) -> b g i", i=NBR)[:, :, i]
                if i == 0:
                    link(nc.vector.tensor_scalar(mask_cs[:], mc, hard[0:NB, 0:1], None, ALU.mult))
                    link(nc.vector.tensor_scalar(mask_rs[:], mask_row[:, :, 0, :], hard[:, 0:1], None, ALU.mult))
                else:
                    link(nc.vector.scalar_tensor_tensor(mask_cs[:], mc, hard[0:NB, i:i + 1], mask_cs[:],
                                                        ALU.mult, ALU.add))
                    link(nc.vector.scalar_tensor_tensor(mask_rs[:], mask_row[:, :, i, :], hard[:, i:i + 1], mask_rs[:],
                                                        ALU.mult, ALU.add))
            for g in range(NMASK):
                link(nc.vector.tensor_scalar(keep["step1"][:, g, :], s1[:], mask_cs[:, g:g + 1], None, ALU.mult))
                link(nc.vector.tensor_tensor(keep["last"][:, g, :], s2[:], mask_rs[:, g, :], ALU.mult))

            for c in range(4):
                dve.wait_ge(filt_dft, c + 1)
                nc.vector.tensor_copy(filt_z[:, 8 * c:8 * c + 8, :].rearrange("p a k -> p (a k)"),
                                      p_f[:, c, 0:8 * NK]).then_inc(filt_saved, 1)

            dve.wait_ge(loaded["sel"], 64)
            for t, rows in enumerate((ROWS_A, ROWS_B)):
                link(nc.vector.tensor_tensor(branch[t][:], branch[t][:], weight[0:rows, :], ALU.mult))
                link(nc.vector.tensor_reduce(keep["w_row"][0:rows, t:t + 1], branch[t][:], AX, ALU.add))
                link(nc.vector.tensor_scalar(keep["select"][t][:], select[t][:], keep["w_row"][0:rows, t:t + 1], None,
                                             ALU.mult))


def norm_and_convolve(nc, d, keep):
    with ExitStack() as own:
        def sb(name, shape, dt=F32):
            return own.enter_context(nc.sbuf_tensor(name, shape, dt))

        def sem(name):
            return own.enter_context(nc.semaphore(name))

        x_in, x_loaded = keep["x_in"], keep["x_loaded"]
        conv_y = sb("conv_y", [128, TOK])
        xc_t = sb("xc_t", [NB, NTOK, TW])
        sq1 = sb("sq1", [NB, NTOK, TW])
        x1_t = sb("x1_t", [NB, NTOK, TW])
        u_t = [sb(f"u_t{i}", [NB, NTOK, TW]) for i in range(2)]
        sq2 = sb("sq2", [NB, NTOK, TW])
        z_sb = sb("z_sb", [NROW, NTOK, TW])
        st1 = sb("st1", [NB, 5, 64])
        st2 = sb("st2", [NB, 6, 64])
        pad = keep["pad"]

        p_cen = own.enter_context(nc.psum_tensor("p_cen", [128, 2, 512], F32))
        p_conv = own.enter_context(nc.psum_tensor("p_conv", [128, 2, 512], F32))
        p_xt = own.enter_context(nc.psum_tensor("p_xt", [128, 2, 512], F32))
        p_rt = own.enter_context(nc.psum_tensor("p_rt", [128, 2, 512], F32))

        peaks_done, row_peak_done = sem("peaks_done"), sem("row_peak_done")
        (cen_ready, conv_ready, xt_ready, rt_ready, z_ready, sign_done, xt_copied, xt_squared, z_saved, y_saved,
         r_done, sq2_done, u_done, ssq1_done, x1_done, u_centered, rstd2_done, x1_stored, z_stored, step) = (
            sem(n) for n in (
                "cen_ready", "conv_ready", "xt_ready", "rt_ready", "z_ready", "sign_done", "xt_copied", "xt_squared",
                "z_saved", "y_saved", "r_done", "sq2_done", "u_done", "ssq1_done", "x1_done", "u_centered",
                "rstd2_done", "x1_stored", "z_stored", "norm_step"))
        sp_turn = sem("sp_turn")

        x_pairs = d["x"].rearrange("(q i) c h w -> q (i c) (h w)", i=2)
        block = own.enter_context(nc.Block())

        @block.sync
        def _(sp):
            def load(q, slot):
                sp.dma_start(x_in[slot][:], x_pairs[q]).then_inc(x_loaded[slot], 16)

            def store_z(q):
                sp.wait_ge(z_saved, NTOK * q + 2 * NTOK)
                after_wait(sp, sp_turn)
                sp.dma_start(d["z"][:, :, bass.ds(q * 128, 128)],
                             z_sb[:].rearrange("p c (a n) -> p (c a) n", n=128)).then_inc(z_stored, 16)

            def body(q, slot, use):
                if not known(q, 0, 1):
                    store_z(q - 2)
                sp.wait_ge(x1_done, NTOK * q + NTOK)
                after_wait(sp, sp_turn)
                sp.dma_start(d["x1"][q], x1_t[:].rearrange("p c n -> p (c n)")).then_inc(x1_stored, 16)
                if not known(q, NPAIR - 2, NPAIR - 1):
                    sp.wait_ge(xt_ready, NTOK * q + NTOK)
                    after_wait(sp, sp_turn)
                    sp.wait_ge(r_done, NCONV * q + NCONV)
                    after_wait(sp, sp_turn)
                    load(q + 2, slot)

            sp.sem_inc(z_stored, 16)
            two_by_two(sp, NPAIR, body, last_apart=2)
            store_z(NPAIR - 2)
            store_z(NPAIR - 1)
            sp.wait_ge(x1_stored, 16 * NPAIR)
            sp.wait_ge(z_stored, 16 * NPAIR + 16)

        @block.tensor
        def _(pe):
            def step1(q, slot, after):
                for c in range(NTOK):
                    if c == 0:
                        pe.wait_ge(sign_done, NCONV * after + NCONV)
                    pe.wait_ge(z_saved, NTOK * q + NTOK + max(c - 1, 0))
                    if c % 2 == 0:
                        pe.wait_ge(u_done, 4 * q + c // 2 + 1)
                    nc.tensor.matmul(p_cen[:, c % 2, :], keep["step1"][:, c // 2, :], u_t[slot][:, c, :],
                                     start=True, stop=True).then_inc(z_ready, 1)

            def center(q, slot, use):
                pe.wait_ge(x_loaded[slot], 16 * use)
                for c in range(NCONV):
                    if c >= 2:
                        pe.wait_ge(sign_done, NCONV * q + c - 1)
                    elif not known(q, 0, 1, 2) and c == 0:
                        pe.wait_ge(z_saved, NTOK * q - NTOK)
                    elif not is_first(q) and c == 0:
                        pe.wait_ge(sign_done, NCONV * q)
                    nc.tensor.matmul(p_cen[:, c % 2, 0:CW], keep["center"][:], x_in[slot][:, CW * c:CW * c + CW],
                                     start=True, stop=True).then_inc(cen_ready, 1)

            def body(q, slot, use):
                x = x_in[slot]
                if is_first(q):
                    center(0, 0, 1)
                for c in range(NTOK):
                    if not (is_first(q) and c < 2):
                        pe.wait_ge(xt_copied, NTOK * q + c - 1)
                        pe.wait_ge(xt_squared, NTOK * q + c - 1)
                    for j in range(ACH):
                        a = ACH * c + j
                        mm = nc.tensor.matmul(p_xt[0:NB, c % 2, 128 * j:128 * j + 128], x[:, a:TOK:NA],
                                              keep["center"][:], start=True, stop=True)
                    mm.then_inc(xt_ready, 1)
                if not known(q, 0, 1):
                    step1(q - 2, slot, q)
                for c in range(NCONV):
                    pe.wait_ge(sign_done, NCONV * q + min(c + 2, NCONV))
                    if not (is_first(q) and c < 2):
                        pe.wait_ge(y_saved, NCONV * q + c - 1)
                    for t in range(9):
                        rows = slice(CROWS * c + t // 3, CROWS * c + t // 3 + CROWS)
                        mm = nc.tensor.matmul(p_conv[:, c % 2, 0:CW], keep["conv_w"][:, t, :],
                                              pad[:, rows, t % 3:t % 3 + WID], start=(t == 0), stop=(t == 8))
                    mm.then_inc(conv_ready, 1)
                if not known(q, NPAIR - 1):
                    center(q + 1, 1 - slot, use + slot)
                pe.wait_ge(r_done, NCONV * q + NCONV)
                for c in range(NTOK):
                    if not (is_first(q) and c < 2):
                        pe.wait_ge(x1_done, NTOK * q + c - 1)
                    for j in range(ACH):
                        a = ACH * c + j
                        mm = nc.tensor.transpose(p_rt[0:NB, c % 2, 128 * j:128 * j + 128], conv_y[:, a:TOK:NA],
                                                 keep["ident"][:])
                    mm.then_inc(rt_ready, 1)

            two_by_two(pe, NPAIR, body, last_apart=2)
            for q in (NPAIR - 2, NPAIR - 1):
                step1(q, q % 2, NPAIR - 1)

        @block.scalar
        def _(act):
            def save_z(q):
                act.wait_ge(z_stored, 16 * q + 16)
                for c in range(NTOK):
                    act.wait_ge(z_ready, NTOK * q + c + 1)
                    nc.scalar.activation(z_sb[:, c, :], p_cen[:, c % 2, :], ACT.Copy).then_inc(z_saved, 1)

            def signs(q):
                if not is_first(q):
                    act.wait_ge(conv_ready, NCONV * q)
                for c in range(NCONV):
                    act.wait_ge(cen_ready, NCONV * q + c + 1)
                    nc.scalar.activation(pad[:, 1 + CROWS * c:1 + CROWS * c + CROWS, 1:1 + WID],
                                         p_cen[:, c % 2, 0:CW].rearrange("p (h w) -> p h w", w=WID),
                                         ACT.Sign).then_inc(sign_done, 1)

            def body(q, slot, use):
                if is_first(q):
                    signs(0)
                if not is_first(q):
                    act.wait_ge(x1_done, NTOK * q)
                for c in range(NTOK):
                    act.wait_ge(xt_ready, NTOK * q + c + 1)
                    nc.scalar.activation(xc_t[:, c, :], p_xt[0:NB, c % 2, :], ACT.Copy).then_inc(xt_copied, 1)
                    if not is_first(q) and c % 4 == 0:
                        act.wait_ge(ssq1_done, 2 * q + c // 4 - 1)
                    nc.scalar.activation(sq1[:, c, :], p_xt[0:NB, c % 2, :], ACT.Square).then_inc(xt_squared, 1)
                if not known(q, 0, 1):
                    save_z(q - 2)
                if not is_first(q):
                    act.wait_ge(rt_ready, NTOK * q)
                for c in range(NCONV):
                    act.wait_ge(conv_ready, NCONV * q + c + 1)
                    nc.scalar.activation(conv_y[:, CW * c:CW * c + CW], p_conv[:, c % 2, 0:CW], ACT.Identity,
                                         bias=keep["bn"][:, 1:2], scale=keep["bn"][:, 0:1]).then_inc(y_saved, 1)
                if not known(q, NPAIR - 1):
                    signs(q + 1)

            act.sem_inc(z_saved, NTOK)
            two_by_two(act, NPAIR, body, last_apart=2)
            save_z(NPAIR - 2)
            save_z(NPAIR - 1)

        @block.gpsimd
        def _(pool):
            def normed(q, slot):
                for c in range(4):
                    pool.wait_ge(rstd2_done, q + 1)
                    v = u_t[slot][:, 2 * c:2 * c + 2, :].rearrange("p c (g n) -> p (c g) n", n=CH)
                    r = st2[:, 3, 16 * c:16 * c + 16].unsqueeze(2).to_broadcast([NB, 16, CH])
                    nc.gpsimd.tensor_tensor(v, v, r, ALU.mult).then_inc(u_done, 1)

            def body(q, slot, use):
                for c in range(NCONV):
                    pool.wait_ge(y_saved, NCONV * q + c + 1)
                    v = conv_y[:, CW * c:CW * c + CW]
                    nc.gpsimd.tensor_tensor(v, v, x_in[slot][:, CW * c:CW * c + CW], ALU.add).then_inc(r_done, 1)
                if not is_first(q):
                    normed(q - 1, 1 - slot)
                for h in range(2):
                    pool.wait_ge(u_centered, 2 * q + h + 1)
                    v = u_t[slot][:, 4 * h:4 * h + 4, :]
                    nc.gpsimd.tensor_tensor(sq2[:, 4 * h:4 * h + 4, :], v, v, ALU.mult).then_inc(sq2_done, 1)

            pool.wait_ge(peaks_done, 2)
            nc.gpsimd.partition_all_reduce(keep["peak"][:], keep["peaks"][:], 128, bass.bass_isa.ReduceOp.max)
            two_by_two(pool, NPAIR, body)
            normed(NPAIR - 1, (NPAIR - 1) % 2)

        @block.vector
        def _(dve):
            STEPS2 = 2 + 1 + RSQRT_STEPS
            STEPS1 = 1 + RSQRT_STEPS + 2 + 2 + 1
            STEPS = STEPS1 + STEPS2 - 1

            def rstd2(q, link):
                for h in range(2):
                    dve.wait_ge(sq2_done, 2 * q + h + 1)
                    link(nc.vector.tensor_reduce(st2[:, 1, 32 * h:32 * h + 32],
                                                 sq2[:, 4 * h:4 * h + 4, :].rearrange("p c (g n) -> p (c g) n", n=CH),
                                                 AX, ALU.add))
                link(nc.vector.tensor_scalar(st2[:, 2, :], st2[:, 1, :], 1.0 / CH, 1e-5, ALU.mult, ALU.add))
                if not is_first(q):
                    dve.wait_ge(u_done, 4 * q)
                rsqrt_steps(nc, link, st2[:, 3, :], st2[:, 2, :], st2[:, 4, :], st2[:, 5, :])

            def body(q, slot, use):
                first = is_first(q)
                base = 0 if first else STEPS1 + (q - 1) * (STEPS1 + 3 + RSQRT_STEPS)
                n = [0]

                def link(ins):
                    n[0] += 1
                    ins.then_inc(step, 1)
                    dve.wait_ge(step, base + n[0])

                for h in range(2):
                    dve.wait_ge(xt_squared, NTOK * q + 4 * h + 4)
                    nc.vector.tensor_reduce(st1[:, 0, 32 * h:32 * h + 32],
                                            sq1[:, 4 * h:4 * h + 4, :].rearrange("p c (g n) -> p (c g) n", n=CH),
                                            AX, ALU.add).then_inc(ssq1_done, 1)
                dve.wait_ge(ssq1_done, 2 * q + 2)
                link(nc.vector.tensor_scalar(st1[:, 1, :], st1[:, 0, :], 1.0 / CH, 1e-6, ALU.mult, ALU.add))
                rsqrt_steps(nc, link, st1[:, 2, :], st1[:, 1, :], st1[:, 3, :], st1[:, 4, :])
                if not first:
                    rstd2(q - 1, link)
                    nc.vector.tensor_copy(st2[:, 4, 0:1], st2[:, 3, 0:1]).then_inc(rstd2_done, 1)
                dve.wait_ge(xt_copied, NTOK * q + NTOK)
                for h in range(2):
                    v = xc_t[:, 4 * h:4 * h + 4, :].rearrange("p c (g n) -> p (c g) n", n=CH)
                    link(nc.vector.tensor_tensor(v, v, st1[:, 2, 32 * h:32 * h + 32].unsqueeze(2)
                                                 .to_broadcast([NB, 32, CH]), ALU.mult))
                if not first:
                    dve.wait_ge(x1_stored, 16 * q)
                for c in range(NTOK):
                    dve.wait_ge(rt_ready, NTOK * q + c + 1)
                    nc.vector.tensor_tensor(x1_t[:, c, :], xc_t[:, c, :], p_rt[0:NB, c % 2, :],
                                            ALU.add).then_inc(x1_done, 1)
                for h in range(2):
                    dve.wait_ge(x1_done, NTOK * q + 4 * h + 4)
                    link(nc.vector.tensor_reduce(st2[:, 0, 32 * h:32 * h + 32],
                                                 x1_t[:, 4 * h:4 * h + 4, :].rearrange("p c (g n) -> p (c g) n", n=CH),
                                                 AX, ALU.add))
                link(nc.vector.tensor_scalar(st2[:, 0, :], st2[:, 0, :], 1.0 / CH, None, ALU.mult))
                if not known(q, 0, 1):
                    dve.wait_ge(z_ready, NTOK * q - NTOK)
                for h in range(2):
                    shape = "p c (g n) -> p (c g) n"
                    nc.vector.tensor_tensor(
                        u_t[slot][:, 4 * h:4 * h + 4, :].rearrange(shape, n=CH),
                        x1_t[:, 4 * h:4 * h + 4, :].rearrange(shape, n=CH),
                        st2[:, 0, 32 * h:32 * h + 32].unsqueeze(2).to_broadcast([NB, 32, CH]),
                        ALU.subtract).then_inc(u_centered, 1)
                assert n[0] == STEPS1 - 0 + (0 if first else 3 + RSQRT_STEPS), n[0]

            STEPS1 = 1 + RSQRT_STEPS + 2 + 3
            dve.wait_ge(keep["m_loaded"], 16 * 3 * NBR)
            for t, rows in enumerate((ROWS_A, ROWS_B)):
                row_peak, w_row = keep["row_peak"][0:rows, t:t + 1], keep["w_row"][0:rows, t:t + 1]
                nc.vector.tensor_reduce(row_peak, keep["m_raw"][t][:], AX, ALU.max,
                                        apply_absolute_value=True).then_inc(row_peak_done, 1)
                dve.wait_ge(row_peak_done, 2 * t + 1)
                nc.vector.scalar_tensor_tensor(row_peak, row_peak, w_row, w_row, ALU.mult,
                                               ALU.mult).then_inc(row_peak_done, 1)
            for t, rows in enumerate((ROWS_A, ROWS_B)):
                dve.wait_ge(row_peak_done, 4)
                nc.vector.tensor_copy(keep["peaks"][0:rows, t:t + 1], keep["row_peak"][0:rows, t:t + 1]).then_inc(peaks_done, 1)
            two_by_two(dve, NPAIR, body)
            n = [STEPS1 + (NPAIR - 1) * (STEPS1 + 3 + RSQRT_STEPS)]

            def link(ins):
                n[0] += 1
                ins.then_inc(step, 1)
                dve.wait_ge(step, n[0])
            rstd2(NPAIR - 1, link)
            nc.vector.tensor_copy(st2[:, 4, 0:1], st2[:, 3, 0:1]).then_inc(rstd2_done, 1)


PLAN = [("x", 4), ("t1", 1), ("h", 2), ("t1", 2), ("h", 2), ("t1", 1), ("h", 2), ("t2", 2), ("h", 2), ("t2", 2),
        ("inv", 4), ("mix", 4)]
TAIL = ("t1", "t2", "inv")
RING = 7


def unit_chunks():
    seen, out = {}, []
    for stage, count in PLAN:
        for _ in range(count):
            k = seen.get(stage, 0)
            seen[stage] = k + 1
            out.append((stage, k, len(out)))
    return out


def chunk_is_there(stage, u):
    return (u > 0) if stage in TAIL else (u < NUNIT)


def chunks_until(u, p, engine=None):
    plan = unit_chunks()
    if isinstance(u, int):
        return sum(1 for w in range(u + 1) for stage, _, at in plan
                   if chunk_is_there(stage, w) and (w < u or at <= p) and engine in (None, at % 2))
    per_unit = sum(1 for _, _, at in plan if engine in (None, at % 2))
    missing = sum(1 for stage, _, at in plan if stage in TAIL and engine in (None, at % 2))
    return per_unit * u - missing + sum(1 for _, _, at in plan if at <= p and engine in (None, at % 2))


def mix_frequencies(nc, d, keep):
    chunks = unit_chunks()
    NCH = len(chunks)
    assert NCH % RING == 0 and NCH % 2 == 0
    pos = {(s, k): p for s, k, p in chunks}
    with ExitStack() as own:
        def sb(name, shape, dt=F32):
            return own.enter_context(nc.sbuf_tensor(name, shape, dt))

        def sem(name):
            return own.enter_context(nc.semaphore(name))

        z_in = [sb(f"z_in{i}", [128, ZCOLS]) for i in range(2)]
        fwd = [sb(f"fwd{i}", [128, 128]) for i in range(2)]
        inv = [sb(f"inv{i}", [128, 2, 128]) for i in range(2)]
        xf = sb("xf", [128, NF, NIMG])
        hf = sb("hf", [128, NF, 2, CH])
        y1 = sb("y1", [128, 8, 2, 2, CH])
        y2 = sb("y2", [128, 16, 2, 2, NALPHA])
        yt = sb("yt", [128, 16, 2, CH])
        wf = sb("wf", [128, 2, 16, CH])
        v_mov = [sb(f"v_mov{i}", [KROWS, NF], F16) for i in range(2)]
        m_sta = [sb(f"m_sta{i}", [KROWS, CH, 128], F16) for i in range(2)]
        sc = sb("sc", [128, 12])
        ring = own.enter_context(nc.psum_tensor("ring", [128, RING, 512], F32))
        p_v = own.enter_context(nc.psum_tensor("p_v", [128, 512], F32))

        z_loaded = [sem(f"z_loaded{i}") for i in range(2)]
        inv_loaded = [sem(f"inv_loaded{i}") for i in range(2)]
        chunk_ready, v_ready, v_saved, w_stored, w_free = (
            sem(n) for n in ("chunk_ready", "v_ready", "v_saved", "w_stored", "w_free"))
        sp_turn, pool_turn = sem("sp_turn"), sem("pool_turn")
        m_ready, m_zeroed, v_high, scaled, scale_step, reals_done = (
            sem(n) for n in ("m_ready", "m_zeroed", "v_high", "scaled", "scale_step", "reals_done"))
        m_saved = [sem("m_high_saved"), sem("m_low_saved")]
        M_CHUNKS = CH * CH // 512
        DCH = 512 // CH
        saved = [sem("saved_by_act"), sem("saved_by_dve")]

        z_units = d["z"].rearrange("(u r) a c -> u (r a) c", r=4)
        w_units = d["w"].rearrange("(u s r) a (h m) e -> u h (r a) s (m e)", s=2, r=2, h=2)
        block = own.enter_context(nc.Block())

        def out_of(stage, k, u_prev):
            def view(bank):
                if stage == "x":
                    return (xf[:, :, 8 * k:8 * k + 8].rearrange("p f i -> p i f"),
                            bank.rearrange("p (i f) -> p i f", f=NF))
                if stage == "mix":
                    return (y1[:, 4 * (k % 2):4 * (k % 2) + 4, :, k // 2, :],
                            bank.rearrange("p (a r e) -> p a r e", r=2, e=CH))
                if stage == "t1":
                    r, part = divmod(k, 2)
                    return (y2[:, :, :, r, 16 * part:16 * part + 16].rearrange("p m h f -> p f h m"),
                            bank.rearrange("p (f h m) -> p f h m", h=2, m=16))
                if stage == "t2":
                    return yt[:, 4 * k:4 * k + 4, :, :].rearrange("p m s e -> p (m s e)"), bank
                g, s = divmod(k, 2)
                return wf[:, s, 8 * g:8 * g + 8, :].rearrange("p m e -> p (m e)"), bank
            return view

        @block.sync
        def _(sp):
            def load(u, slot):
                sp.dma_start(z_in[slot][:], z_units[u]).then_inc(z_loaded[slot], 16)
                sp.dma_start(fwd[slot][:], d["c_fwd"][u]).then_inc(z_loaded[slot], 16)

            def load_inv(u, slot):
                sp.dma_start(inv[slot][:].rearrange("p n f -> p (n f)"), d["c_inv"][u]).then_inc(inv_loaded[slot], 16)

            def body(u, slot, use):
                if not known(u, NUNIT - 1):
                    if not is_first(u):
                        sp.wait_ge(chunk_ready, chunks_until(u - 1, pos["mix", 3]))
                        after_wait(sp, sp_turn)
                    load(u + 1, 1 - slot)
                    if not is_first(u):
                        sp.wait_ge(chunk_ready, chunks_until(u, pos["inv", 3]))
                        after_wait(sp, sp_turn)
                    load_inv(u + 1, 1 - slot)

            load(0, 0)
            load_inv(0, 0)
            two_by_two(sp, NUNIT, body, last_apart=2)

        @block.gpsimd
        def _(pool):
            def store(u):
                for e in range(2):
                    pool.wait_ge(saved[e], chunks_until(u + 1, pos["inv", 3], e))
                after_wait(pool, pool_turn)
                for h in range(2):
                    nc.gpsimd.dma_start(w_units[u, h], wf[64 * h:64 * h + 64].rearrange("p s m e -> p s (m e)")).then_inc(w_stored, 16)
                pool.wait_ge(w_stored, 32 * (u + 1))
                pool.sem_inc(w_free, 1)

            pool.sem_inc(w_free, 1)
            for part in m_sta:
                nc.gpsimd.memset(part[:].rearrange("k e n -> k (e n)").bitcast(F32), 0.0).then_inc(m_zeroed, 1)
            for part in v_mov:
                nc.gpsimd.memset(part[:].bitcast(F32), 0.0).then_inc(m_zeroed, 1)

            store(0)
            with pool.Fori(1, NUNIT - 1) as u:
                store(u)
            store(NUNIT - 1)

        def bank_free(eng, u, p):
            if not isinstance(u, int):
                w, at = (u, p - RING) if p >= RING else (u - 1, p - RING + NCH)
                eng.wait_ge(saved[at % 2], chunks_until(w, at, at % 2))
                return
            before = [(w, at) for w in range(u + 1) for stage, _, at in chunks
                      if chunk_is_there(stage, w) and at % RING == p % RING and (w < u or at < p)]
            if before:
                w, at = before[-1]
                eng.wait_ge(saved[at % 2], chunks_until(w, at, at % 2))

        def all_saved(eng, u, p):
            for e in range(2):
                eng.wait_ge(saved[e], chunks_until(u, p, e))

        @block.tensor
        def _(pe):
            def unit(u, slot, use, head, tail):
                if head:
                    pe.wait_ge(z_loaded[slot], 32 * use)
                    if not is_first(u):
                        pe.wait_ge(v_saved, 2 * u)
                    lhs = z_in[slot][:, NIMG * CH:ZCOLS]
                    nc.tensor.matmul(p_v[0:NK, 0:NF], lhs, fwd[slot][:, 0:NF], start=True, stop=True)
                    nc.tensor.matmul(p_v[KI:KROWS, 0:NF], lhs, fwd[slot][:, NF:2 * NF], start=True,
                                     stop=True).then_inc(v_ready, 1)
                for stage, k, p in chunks:
                    if not (tail if stage in TAIL else head):
                        continue
                    bank_free(pe, u, p)
                    bank = ring[:, p % RING, :]
                    if stage == "x":
                        for i in range(8):
                            z = z_in[slot][:, CH * (8 * k + i):CH * (8 * k + i) + CH]
                            for r in range(2):
                                mm = nc.tensor.matmul(bank[CH * r:CH * r + CH, NF * i:NF * i + NF], z,
                                                      fwd[slot][:, NF * r:NF * r + NF], start=True, stop=True)
                    elif stage == "h":
                        if k == 0:
                            pe.wait_ge(v_saved, 2 * u + 2)
                        for i in range(8):
                            for n, (m, v) in enumerate(((0, 0), (0, 1), (1, 0))):
                                mm = nc.tensor.matmul(bank[:, NF * i:NF * i + NF], m_sta[m][:, 8 * k + i, :],
                                                      v_mov[v][:], start=(n == 0), stop=(n == 2))
                    elif stage == "mix":
                        if k == 0:
                            all_saved(pe, u, pos["h", 7])
                            if is_first(u):
                                pe.wait_ge(reals_done, 3)
                        for i in range(4):
                            for j in range(4):
                                f = 16 * k + 4 * i + j
                                mm = nc.tensor.matmul(bank[32 * j:32 * j + 32, 128 * i:128 * i + 128], xf[:, f, :],
                                                      hf[:, f, :, :].rearrange("p r e -> p (r e)"),
                                                      start=True, stop=True, tile_position=(0, 32 * j))
                    elif stage == "t1":
                        if k == 0:
                            all_saved(pe, u - 1, pos["mix", 3])
                        r, part = divmod(k, 2)
                        for i in range(4):
                            mm = nc.tensor.transpose(bank[:, 128 * i:128 * i + 128],
                                                     y1[:, 4 * part + i, r, :, :].rearrange("p s e -> p (s e)"),
                                                     keep["ident"][:])
                    elif stage == "t2":
                        if k == 0:
                            all_saved(pe, u, pos["t1", 3])
                        for i in range(4):
                            mm = nc.tensor.transpose(bank[:, 128 * i:128 * i + 128],
                                                     y2[:, 4 * k + i, :, :, :].rearrange("p h r f -> p (h r f)"),
                                                     keep["ident"][:])
                    else:
                        g, s = divmod(k, 2)
                        if s == 0:
                            all_saved(pe, u, pos["t2", 2 * g + 1])
                        if k == 0:
                            pe.wait_ge(inv_loaded[1 - slot], 16 * (use if slot else use - 1))
                        mm = nc.tensor.matmul(bank, inv[1 - slot][:, s, :], yt[:, 8 * g:8 * g + 8, s, :],
                                              start=True, stop=True)
                    mm.then_inc(chunk_ready, 1)

            def body(u, slot, use):
                unit(u, slot, use, True, not is_first(u))

            for c in range(M_CHUNKS):
                if c >= RING:
                    for e in range(2):
                        pe.wait_ge(m_saved[e], 2 * (c - RING + 1))
                for t in range(2):
                    mm = nc.tensor.matmul(ring[0:KROWS, c % RING, :], keep["select"][t][:],
                                          keep["m_raw"][t][:, 512 * c:512 * c + 512], start=(t == 0), stop=(t == 1))
                mm.then_inc(m_ready, 1)
            for e in range(2):
                pe.wait_ge(m_saved[e], 2 * M_CHUNKS)

            two_by_two(pe, NUNIT, body)
            unit(NUNIT, 0, NUNIT // 2 + 1, False, True)

        def m_part(n, copy_of, c):
            at = KI * copy_of
            return (m_sta[n][at:at + NK, :, CH * copy_of + DCH * c:CH * copy_of + DCH * c + DCH]
                    .rearrange("k e d -> k d e"),
                    ring[at:at + NK, c % RING, :].rearrange("k (d e) -> k d e", e=CH))

        def saver(eng, which, copy):
            def unit(u, head, tail):
                if head and which:
                    eng.wait_ge(v_ready, u + 1)
                    for at in (0, KI):
                        nc.vector.tensor_scalar(v_mov[0][at:at + NK, :], p_v[at:at + NK, 0:NF],
                                                sc[at:at + NK, V_SCALE:V_SCALE + 1], None, ALU.mult).then_inc(v_high, 1)
                    eng.wait_ge(v_high, 2 * u + 2)
                    for at in (0, KI):
                        nc.vector.scalar_tensor_tensor(v_mov[1][at:at + NK, :], p_v[at:at + NK, 0:NF],
                                                       sc[at:at + NK, V_SCALE:V_SCALE + 1], v_mov[0][at:at + NK, :],
                                                       ALU.mult, ALU.subtract).then_inc(v_saved, 1)
                for stage, k, p in chunks:
                    if p % 2 != which or not (tail if stage in TAIL else head):
                        continue
                    eng.wait_ge(chunk_ready, chunks_until(u, p))
                    bank = ring[:, p % RING, :]
                    if stage == "inv" and k < 2:
                        eng.wait_ge(w_free, u)
                    if stage == "h":
                        src = bank.rearrange("p (e f) -> p e f", f=NF)
                        e8 = slice(8 * k, 8 * k + 8)
                        copy(hf[:, :, 0, e8].rearrange("p f e -> p e f"), src)
                        copy(hf[0:CH, :, 1, e8].rearrange("p f e -> p e f"), src[CH:2 * CH], -1.0)
                        copy(hf[CH:2 * CH, :, 1, e8].rearrange("p f e -> p e f"), src[0:CH]).then_inc(saved[which], 1)
                    else:
                        dst, src = out_of(stage, k, u)(bank)
                        copy(dst, src).then_inc(saved[which], 1)
                    if is_first(u) and (stage, k) == ("h", 7) and which:
                        for e in range(2):
                            eng.wait_ge(saved[e], chunks_until(u, pos["h", 7], e))
                        nc.vector.tensor_scalar(hf[CH:2 * CH, 0, 1, :], hf[CH:2 * CH, 0, 0, :], -1.0, None,
                                                ALU.mult).then_inc(reals_done, 1)
                        nc.vector.memset(hf[0:CH, 0, 1, :], 0.0).then_inc(reals_done, 1)
                        eng.wait_ge(reals_done, 1)
                        nc.vector.memset(hf[CH:2 * CH, 0, 0, :], 0.0).then_inc(reals_done, 1)

            return unit

        M_SCALE, V_SCALE, UNSCALE = 8, 9, 10

        @block.scalar
        def _(act):
            def copy(dst, src, scale=1.0):
                return nc.scalar.activation(dst, src, ACT.Copy, scale=scale)

            act.wait_ge(m_zeroed, 2)
            act.wait_ge(scaled, 1)
            for c in range(M_CHUNKS):
                act.wait_ge(m_ready, c + 1)
                for copy_of in range(2):
                    dst, src = m_part(0, copy_of, c)
                    nc.scalar.activation(dst, src, ACT.Copy, scale=sc[KI * copy_of:KI * copy_of + NK, M_SCALE:M_SCALE + 1]
                                         ).then_inc(m_saved[0], 1)
            unit = saver(act, 0, copy)
            two_by_two(act, NUNIT, lambda u, slot, use: unit(u, True, not is_first(u)))
            unit(NUNIT, False, True)

        @block.vector
        def _(dve):
            def copy(dst, src, scale=None):
                if scale is None:
                    return nc.vector.tensor_copy(dst, src)
                return nc.vector.tensor_scalar(dst, src, scale, None, ALU.mult)

            n = [0]

            def link(ins):
                n[0] += 1
                ins.then_inc(scale_step, 1)
                dve.wait_ge(scale_step, n[0])

            link(nc.vector.tensor_tensor(sc[:, 0:1], keep["peak"][:, 0:1], keep["peak"][:, 1:2], ALU.max))
            link(nc.vector.tensor_scalar(sc[:, 1:2], keep["peak"][:, 2:3], float(PHI_LEN), 1.0, ALU.mult, ALU.max))
            link(nc.vector.tensor_scalar(sc[:, 0:1], sc[:, 0:1], 2.0 * NBR, 1e-30, ALU.mult, ALU.max))
            link(nc.vector.tensor_scalar(sc[:, 2:4].bitcast(I32), sc[:, 0:2].bitcast(I32), EXPONENT, None,
                                         ALU.bitwise_and))
            link(nc.vector.tensor_scalar(sc[:, 8:10].bitcast(I32), sc[:, 2:4].bitcast(I32), -1.0,
                                         float((2 * 127 + HALF_TOP) << 23), ALU.mult, ALU.add))
            nc.vector.memset(sc[:, 11:12], 0.0).then_inc(scaled, 1)
            link(nc.vector.scalar_tensor_tensor(sc[:, 10:11], sc[:, 2:3], 2.0 ** (-2 * HALF_TOP), sc[:, 3:4],
                                                ALU.mult, ALU.mult))
            link(nc.vector.tensor_scalar(keep["last"][:], keep["last"][:], sc[:, UNSCALE:UNSCALE + 1], None, ALU.mult))
            dve.wait_ge(m_zeroed, 4)
            for c in range(M_CHUNKS):
                dve.wait_ge(m_saved[0], 2 * c + 2)
                for copy_of in range(2):
                    dst, src = m_part(1, copy_of, c)
                    nc.vector.scalar_tensor_tensor(dst, src, sc[KI * copy_of:KI * copy_of + NK, M_SCALE:M_SCALE + 1],
                                                   m_part(0, copy_of, c)[0], ALU.mult, ALU.subtract
                                                   ).then_inc(m_saved[1], 1)
            unit = saver(dve, 1, copy)
            two_by_two(dve, NUNIT, lambda u, slot, use: unit(u, True, not is_first(u)))
            unit(NUNIT, False, True)


def finish(nc, d, keep):
    with ExitStack() as own:
        def sb(name, shape, dt=F32):
            return own.enter_context(nc.sbuf_tensor(name, shape, dt))

        def sem(name):
            return own.enter_context(nc.semaphore(name))

        w_in = [sb(f"w_in{i}", [NROW, NA, 128]) for i in range(2)]
        x1_in = [sb(f"x1_in{i}", [NB, NA, 128]) for i in range(2)]
        out_sb = [sb(f"out_sb{i}", [128, NB, NA]) for i in range(2)]
        p_out = own.enter_context(nc.psum_tensor("p_out", [128, 4, 512], F32))
        p_x1 = own.enter_context(nc.psum_tensor("p_x1", [128, 4, 512], F32))
        w_loaded = [sem(f"w_loaded{i}") for i in range(2)]
        out_stored = [sem(f"out_stored{i}") for i in range(2)]
        out_ready, x1_ready, x1_saved, summed = (sem(n) for n in ("out_ready", "x1_ready", "x1_saved", "out_summed"))
        sp_turn, pool_turn = sem("sp_turn"), sem("pool_turn")
        w_rows = d["w"].rearrange("r a i e -> r a (i e)")
        out_pairs = d["out"].rearrange("(q i) c h w -> q (i c) (h w)", i=2)
        BANKS = 4
        block = own.enter_context(nc.Block())

        def tokens(slot, c):
            return out_sb[slot][:, :, ACH * c:ACH * c + ACH].rearrange("p b a -> p a b")

        def view(bank):
            return bank[:, 0:ACH * NB].rearrange("p (a b) -> p a b", b=NB)

        @block.sync
        def _(sp):
            def load(q, slot):
                sp.dma_start(w_in[slot][:], w_rows[:, :, bass.ds(q * 128, 128)]).then_inc(w_loaded[slot], 16)
                sp.dma_start(x1_in[slot][:].rearrange("p a n -> p (a n)"), d["x1"][q]).then_inc(w_loaded[slot], 16)

            def body(q, slot, use):
                if not known(q, NPAIR - 1):
                    if not is_first(q):
                        sp.wait_ge(out_ready, NTOK * q)
                        after_wait(sp, sp_turn)
                    load(q + 1, 1 - slot)

            load(0, 0)
            two_by_two(sp, NPAIR, body, last_apart=2)

        @block.gpsimd
        def _(pool):
            def body(q, slot, use):
                pool.wait_ge(summed, NTOK * q + NTOK)
                after_wait(pool, pool_turn)
                nc.gpsimd.dma_start(out_pairs[q], out_sb[slot][:].rearrange("p b a -> p (b a)")).then_inc(out_stored[slot], 16)

            two_by_two(pool, NPAIR, body)
            for s in range(2):
                pool.wait_ge(out_stored[s], 16 * (NPAIR // 2))

        @block.tensor
        def _(pe):
            def body(q, slot, use):
                pe.wait_ge(w_loaded[slot], 32 * use)
                for c in range(NTOK):
                    if not (is_first(q) and c < BANKS):
                        pe.wait_ge(x1_saved, NTOK * q + c + 1 - BANKS)
                    for j in range(ACH):
                        mm = nc.tensor.transpose(p_x1[:, c % BANKS, NB * j:NB * j + NB], x1_in[slot][:, ACH * c + j, :],
                                                 keep["ident"][0:NB, 0:NB])
                    mm.then_inc(x1_ready, 1)
                    if not (is_first(q) and c < BANKS):
                        pe.wait_ge(summed, NTOK * q + c + 1 - BANKS)
                    for j in range(ACH):
                        a = ACH * c + j
                        mm = nc.tensor.matmul(p_out[:, c % BANKS, NB * j:NB * j + NB], w_in[slot][:, a, :],
                                              keep["last"][:, a // MASKG, :], start=True, stop=True)
                    mm.then_inc(out_ready, 1)

            two_by_two(pe, NPAIR, body)

        @block.scalar
        def _(act):
            def body(q, slot, use):
                if not known(q, 0, 1):
                    act.wait_ge(out_stored[slot], 16 * (use - 1))
                for c in range(NTOK):
                    act.wait_ge(x1_ready, NTOK * q + c + 1)
                    nc.scalar.activation(tokens(slot, c), view(p_x1[:, c % BANKS, :]), ACT.Copy).then_inc(x1_saved, 1)

            two_by_two(act, NPAIR, body)

        @block.vector
        def _(dve):
            def body(q, slot, use):
                for c in range(NTOK):
                    dve.wait_ge(x1_saved, NTOK * q + c + 1)
                    dve.wait_ge(out_ready, NTOK * q + c + 1)
                    to = tokens(slot, c)
                    nc.vector.tensor_tensor(to, view(p_out[:, c % BANKS, :]), to, ALU.add).then_inc(summed, 1)

            two_by_two(dve, NPAIR, body)


def build(nc, d):
    d["z"] = nc.dram_tensor("z_scratch", [NROW, NA, ZCOLS], F32).ap()
    d["w"] = nc.dram_tensor("w_scratch", [NROW, NA, NIMG, CH], F32).ap()
    d["x1"] = nc.dram_tensor("x1_scratch", [NPAIR, NB, NA * 128], F32).ap()
    with ExitStack() as ctx:
        def sb(name, shape, dt=F32):
            return ctx.enter_context(nc.sbuf_tensor(name, shape, dt))

        keep = {
            "ident": sb("ident", [128, 128]),
            "center": sb("center", [128, 128]),
            "bn": sb("bn_scale_bias", [128, 2]),
            "conv_w": sb("conv_w", [128, 9, 128], BF16),
            "step1": sb("step1_masked", [NB, NMASK, NROW]),
            "last": sb("last_masked", [NROW, NMASK, NB]),
            "m_raw": [sb("m_raw_a", [ROWS_A, CH * CH]), sb("m_raw_b", [ROWS_B, CH * CH])],
            "select": [sb("select_weighted_a", [ROWS_A, KROWS]), sb("select_weighted_b", [ROWS_B, KROWS])],
            "w_row": sb("w_row", [ROWS_A, 2]),
            "row_peak": sb("row_peak", [ROWS_A, 2]),
            "peaks": sb("peaks", [128, 3]),
            "peak": sb("peak", [128, 3]),
            "m_loaded": ctx.enter_context(nc.semaphore("m_loaded")),
            "pad": sb("signs_padded", [128, HGT + 2, WID + 2], BF16),
        }
        with ExitStack() as early:
            keep["x_in"] = [early.enter_context(nc.sbuf_tensor(f"x_in{i}", [128, TOK], F32)) for i in range(2)]
            keep["x_loaded"] = [early.enter_context(nc.semaphore(f"x_loaded{i}")) for i in range(2)]
            prepare(nc, d, keep)
            norm_and_convolve(nc, d, keep)
        mix_frequencies(nc, d, keep)
        finish(nc, d, keep)


_INS = {
    "x": "x", "L0_conv_weight": "weight", "L0_conv_gamma": "gamma", "L0_conv_beta": "beta",
    "L0_conv_bn_mean": "bn_mean", "L0_conv_bn_var": "bn_var", "L0_ffn_sigma": "sigma", "L0_ffn_phi": "phi",
    "L0_ffn_M_u": "M_u", "L0_ffn_M_phi_plus": "M_plus", "L0_ffn_M_phi_minus": "M_minus",
    "L0_ffn_log_weights": "log_weights", "L0_ffn_gumbel": "gumbel",
}


def kernel(**inputs):
    import concourse.bacc as _bacc
    from concourse.bass_utils import run_bass_kernel_spmd as _run

    nc = _bacc.Bacc("TRN2", target_bir_lowering=False, num_devices=1)
    arrays, d = {}, {}
    given = {short: np.ascontiguousarray(inputs[name]) for name, short in _INS.items()}
    for name, a in {**given, **constants()}.items():
        arrays["in_" + name] = a
        d[name] = nc.dram_tensor("in_" + name, a.shape, mybir.dt.from_np(a.dtype), kind="ExternalInput").ap()
    d["out"] = nc.dram_tensor("out_dram", given["x"].shape, F32, kind="ExternalOutput").ap()
    build(nc, d)
    r = _run(nc, [arrays], core_ids=[0])
    return r.results[0]["out_dram"]
```

```python
from contextlib import ExitStack

import numpy as np

import concourse.bass as bass
from concourse import mybir

F32 = mybir.dt.float32
BF16 = mybir.dt.bfloat16
F16 = mybir.dt.float16
I32 = mybir.dt.int32
ALU = mybir.AluOpType
ACT = mybir.ActivationFunctionType
AX = mybir.AxisListType.X

NIMG, CH, HGT, WID = 32, 64, 56, 56
TOK = HGT * WID
NBR = 4
KF, KU = 16, 3
PHI_LEN = 2048
NFFT = 4096

NA = 32
NB = TOK // NA
NSLOT = 64
NALPHA = 32
NROW = 2 * NSLOT
NUNIT = NSLOT // 2
NF = 2 * NALPHA
NK = 2 * KF + KU
KI = 64
KROWS = KI + NK
NPAIR = NIMG // 2
PREFETCHED = (0, 1, NPAIR - 2, NPAIR - 1)
ZCOLS = NIMG * CH + NK

CROWS = 8
NCONV = HGT // CROWS
CW = CROWS * WID
ACH = 4
NTOK = NA // ACH
HALF = NTOK // 2
TW = ACH * 2 * CH
MASKG = 8
NMASK = NA // MASKG

ROWS_A = (NBR - 1) * NK
ROWS_B = NK
M_COLS = CH * CH
M_PIECES = ((0, 0, ROWS_A, 0), (1, 0, ROWS_B, ROWS_A), (1, KI, ROWS_B, ROWS_A))
HALF_TOP = 14
EXPONENT = 0x7F800000
RSQRT_MAGIC = 0x5F3759DF
NEWTON = 3


def slot_frequencies(s):
    if s:
        return [s + 128 * al for al in range(NALPHA)]
    return [128 * al for al in range(16)] + [64 + 128 * al for al in range(16)]


def constants():
    b = np.arange(NB)
    s1 = np.zeros((NB, NROW))
    s2 = np.zeros((NROW, NB))
    s1[:, 0], s1[:, 1] = 1.0, (-1.0) ** b
    s2[0], s2[1] = 1.0, (-1.0) ** b
    for s in range(1, NSLOT):
        th = 2 * np.pi * s * b / 128
        s1[:, 2 * s], s1[:, 2 * s + 1] = np.cos(th), -np.sin(th)
        s2[2 * s], s2[2 * s + 1] = np.cos(th), -np.sin(th)

    a = np.arange(NA)[:, None]
    fwd = np.zeros((NUNIT, 2, 2, NA, 2, 2, NALPHA))
    inv = np.zeros((NUNIT, 2, 2, 2, NALPHA, NA))
    for s in range(NSLOT):
        u, sl = divmod(s, 2)
        f = np.array(slot_frequencies(s))[None, :]
        th = 2 * np.pi * f * a / NFFT
        c, sn = np.cos(th), np.sin(th)
        re_re, re_im, im_re, im_im = c.copy(), -sn, sn.copy(), c.copy()
        ci, si = 2 * c.T / NFFT, 2 * sn.T / NFFT
        g = np.array([[ci, si], [-si, ci]])
        if s == 0:
            z = np.zeros((NA, 16))
            re_re = np.hstack([c[:, :16], z])
            re_im = np.hstack([-sn[:, :16], z])
            im_re = np.hstack([z, c[:, 16:]])
            im_im = np.hstack([z, -sn[:, 16:]])
            re_im[:, 0] = (-1.0) ** a[:, 0]
            g[:] = 0.0
            g[0, 0, :16], g[1, 0, :16] = ci[:16], -si[:16]
            g[0, 1, 16:], g[1, 1, 16:] = ci[16:], -si[16:]
            g[0, 0, 0] = 1.0 / NFFT
            g[1, 0, 0] = (-1.0) ** a[:, 0] / NFFT
        x = np.array([[re_re, re_im], [im_re, im_im]])
        fwd[u, sl, :, :, :, sl] = x.transpose(0, 2, 1, 3)
        inv[u, sl] = g
    fwd = fwd.reshape(NUNIT, 128, 128)
    ib = np.zeros((NUNIT, 2, 2, NALPHA, 2, 2, 2, NA))
    for h in range(2):
        ib[:, h, :, :, :, h] = inv.transpose(0, 2, 4, 1, 3, 5)
    inv = ib.reshape(NUNIT, 128, 2 * 128)

    center = np.kron(np.eye(2), np.eye(CH) - 1.0 / CH)
    t = (np.arange(NMASK) * MASKG)[None, :] + NA * b[:, None]
    mask = np.stack([t < (TOK >> i) for i in range(NBR)], -1)
    mask_col = mask.reshape(NB, NMASK * NBR)
    mask_row = np.broadcast_to(mask.transpose(1, 2, 0).reshape(1, -1), (128, NMASK * NBR * NB))
    sign_a = np.broadcast_to((-1.0) ** np.arange(NA), (KI, NA))
    eye = np.tile(np.eye(NK), (NBR, 1))
    select = np.zeros((NBR * NK, KROWS))
    select[:, 0:NK], select[:, KI:KROWS] = eye, -eye
    branch = np.repeat(np.eye(NBR), NK, 0)
    out = {
        "c_select": select, "c_branch": branch,
        "c_step1": s1, "c_step_last": s2, "c_fwd": fwd, "c_inv": inv, "c_center": center,
        "c_ident": np.eye(128), "c_mask_col": mask_col, "c_mask_row": mask_row, "c_sign_a": sign_a,
    }
    return {k: np.ascontiguousarray(v, dtype=np.float32) for k, v in out.items()}


def rsqrt_guess(nc, link, y, v, t):
    link(nc.vector.tensor_scalar(t.bitcast(I32), v.bitcast(I32), 1, None, ALU.logical_shift_right))
    link(nc.vector.tensor_scalar(y.bitcast(I32), t.bitcast(I32), -1.0, float(RSQRT_MAGIC), ALU.mult, ALU.add))


def rsqrt_steps(nc, link, y, v, t0, t1):
    rsqrt_guess(nc, link, y, v, t0)
    rsqrt_newton(nc, link, y, v, t0, t1)


def rsqrt_newton(nc, link, y, v, t0, t1):
    for _ in range(NEWTON):
        link(nc.vector.tensor_tensor(t0, y, y, ALU.mult))
        link(nc.vector.scalar_tensor_tensor(t1, t0, -0.5, v, ALU.mult, ALU.mult))
        link(nc.vector.scalar_tensor_tensor(y, t1, 1.5, y, ALU.add, ALU.mult))


def rsqrt_refine(nc, link, y, minus_half_v, three_halves, t0):
    for _ in range(NEWTON):
        link(nc.gpsimd.tensor_tensor(t0, y, y, ALU.mult))
        link(nc.gpsimd.tensor_tensor(t0, t0, minus_half_v, ALU.mult))
        link(nc.gpsimd.tensor_tensor(t0, t0, three_halves, ALU.add))
        link(nc.gpsimd.tensor_tensor(y, y, t0, ALU.mult))


RSQRT_STEPS = 2 + 3 * NEWTON
REFINE_STEPS = 4 * NEWTON


def two_by_two(eng, count, body, last_apart=0):
    body(0, 0, 1)
    body(1, 1, 1)
    with eng.Fori(1, (count - last_apart) // 2) as h:
        body(2 * h, 0, h + 1)
        body(2 * h + 1, 1, h + 1)
    for n in range(count - last_apart, count):
        body(n, n % 2, n // 2 + 1)


def known(n, *values):
    return isinstance(n, int) and n in values


def after_wait(eng, sem):
    eng.sem_inc(sem, 1)


def is_first(n):
    return known(n, 0)


def prepare(nc, d, keep):
    with ExitStack() as own:
        def sb(name, shape, dt=F32):
            return own.enter_context(nc.sbuf_tensor(name, shape, dt))

        def sem(name):
            return own.enter_context(nc.semaphore(name))

        w_raw = sb("w_raw", [128, CH * 9])
        w_diag = sb("w_diag", [128, 9, 128])
        bn = sb("bn", [128, 16])
        mix = sb("mix", [128, 64])
        s1 = sb("s1", [NB, NROW])
        s2 = sb("s2", [NROW, NB])
        mask_col = sb("mask_col", [NB, NMASK * NBR])
        mask_row = sb("mask_row", [128, NMASK, NBR, NB])
        mask_cs = sb("mask_cs", [NB, NMASK])
        mask_rs = sb("mask_rs", [128, NMASK, NB])
        sgn_a = sb("sgn_a", [KI, NA])
        phi = sb("phi", [KI, NA, KF])
        sig = sb("sig", [KI, 3, KF])
        filt = sb("filt", [KI, NA, NK])
        filt_z = sb("filt_z", [NROW, NA, NK])
        select = [sb("select_a", [ROWS_A, KROWS]), sb("select_b", [KROWS, KROWS])]
        branch = [sb("branch_a", [ROWS_A, NBR]), sb("branch_b", [KROWS, NBR])]
        p_w = own.enter_context(nc.psum_tensor("p_w", [128, 4, 512], F32))
        p_f = own.enter_context(nc.psum_tensor("p_f", [128, 4, 512], F32))

        loaded = {n: sem("loaded_" + n) for n in ("conv", "bn", "mix", "mask", "step1", "phi", "const", "sel")}
        zeroed, signed, turned = sem("zeroed"), sem("signed"), sem("turned")
        pow_done, exp_in, exp_done = sem("pow_done"), sem("exp_in"), sem("exp_done")
        step, filt_ready, filt_dft, filt_saved, filt_stored = (
            sem(n) for n in ("prep_step", "filt_ready", "filt_dft", "filt_saved", "filt_stored"))

        block = own.enter_context(nc.Block())

        @block.sync
        def _(sp):
            sp.dma_start(sig[:, 0, :], d["sigma"].partition_broadcast(KI)).then_inc(loaded["phi"], 16)
            sp.dma_start(phi[:], d["phi"].rearrange("(b a) k -> b a k", a=NA)).then_inc(loaded["phi"], 16)
            sp.dma_start(sgn_a[:], d["c_sign_a"]).then_inc(loaded["phi"], 16)
            sp.dma_start(s1[:], d["c_step1"]).then_inc(loaded["step1"], 16)
            for h in range(2):
                half = slice(CH * h, CH * h + CH)
                sp.dma_start(w_raw[half, :], d["weight"].rearrange("o i h w -> o (i h w)")).then_inc(loaded["conv"], 16)
                for n, name in enumerate(("gamma", "beta", "bn_mean", "bn_var")):
                    sp.dma_start(bn[half, n:n + 1], d[name].rearrange("(o a) -> o a", a=1)).then_inc(loaded["bn"], 16)
            sp.dma_start(keep["ident"][:], d["c_ident"]).then_inc(loaded["const"], 16)
            sp.dma_start(keep["center"][:], d["c_center"]).then_inc(loaded["const"], 16)
            sp.dma_start(mix[:, 0:4], d["log_weights"].partition_broadcast(128)).then_inc(loaded["mix"], 16)
            sp.dma_start(mix[:, 4:8], d["gumbel"].partition_broadcast(128)).then_inc(loaded["mix"], 16)
            sp.dma_start(s2[:], d["c_step_last"]).then_inc(loaded["mask"], 16)
            sp.dma_start(mask_col[:], d["c_mask_col"]).then_inc(loaded["mask"], 16)
            sp.dma_start(mask_row[:].rearrange("p g i b -> p (g i b)"), d["c_mask_row"]).then_inc(loaded["mask"], 16)
            for t, at, rows, of in M_PIECES:
                sp.dma_start(select[t][at:at + rows, :], d["c_select"][of:of + rows, :]).then_inc(loaded["sel"], 16)
                sp.dma_start(branch[t][at:at + rows, :], d["c_branch"][of:of + rows, :]).then_inc(loaded["sel"], 16)
            x_pairs = d["x"].rearrange("(q i) c h w -> q (i c) (h w)", i=2)
            for q in range(2):
                sp.dma_start(keep["x_in"][q][:], x_pairs[q]).then_inc(keep["x_loaded"][q], 16)
            sp.wait_ge(filt_saved, 4)
            sp.dma_start(d["z"][:, :, NIMG * CH:ZCOLS], filt_z[:]).then_inc(filt_stored, 16)
            for row, n, src in ((0, KF, d["M_plus"]), (KF, KF, d["M_minus"]), (2 * KF, KU, d["M_u"])):
                for i in range(NBR):
                    rows, m = slice(i * NK + row, i * NK + row + n), src[i].rearrange("k d e -> k (d e)")
                    if i < NBR - 1:
                        sp.dma_start(keep["m_raw"][0][rows, :], m).then_inc(keep["m_loaded"], 16)
                    else:
                        for h in range(2):
                            sp.dma_start(keep["m_raw"][1][KI * h + row:KI * h + row + n, :],
                                         m[:, h * M_COLS // 2:(h + 1) * M_COLS // 2]).then_inc(keep["m_loaded"], 16)
            sp.wait_ge(filt_stored, 16)

        @block.gpsimd
        def _(pool):
            nc.gpsimd.memset(sig[:, 1, :], 0.25).then_inc(zeroed, 1)
            pool.wait_ge(zeroed, 1)
            pool.wait_ge(loaded["phi"], 48)
            nc.gpsimd.tensor_tensor(sig[:, 2, :], sig[:, 0, :], sig[:, 1, :], ALU.pow).then_inc(pow_done, 1)
            nc.gpsimd.memset(keep["pad"][:], 0.0)
            nc.gpsimd.memset(keep["peaks"][:], 0.0).then_inc(zeroed, 1)

        @block.scalar
        def _(act):
            act.wait_ge(loaded["conv"], 32)
            act.wait_ge(step, 1)
            for h in range(2):
                half = slice(CH * h, CH * h + CH)
                nc.scalar.activation(w_diag[half, :, half], w_raw[half, :].rearrange("o (i t) -> o t i", t=9),
                                     ACT.Sign).then_inc(signed, 1)
            act.wait_ge(exp_in, 1)
            nc.scalar.activation(mix[:, 12:16], mix[:, 12:16], ACT.Exp).then_inc(exp_done, 1)

        @block.tensor
        def _(pe):
            pe.wait_ge(loaded["step1"], 16)
            pe.wait_ge(filt_ready, 1)
            for c in range(4):
                nc.tensor.matmul(p_f[:, c, 0:8 * NK], s1[0:KI, :], filt[:, 8 * c:8 * c + 8, :],
                                 start=True, stop=True).then_inc(filt_dft, 1)
            pe.wait_ge(loaded["const"], 32)
            pe.wait_ge(signed, 2)
            for t in range(9):
                mm = nc.tensor.transpose(p_w[:, t // 4, 128 * (t % 4):128 * (t % 4) + 128], w_diag[:, t, :],
                                         keep["ident"][:])
            mm.then_inc(turned, 1)

        @block.vector
        def _(dve):
            n = [0]

            def link(ins):
                n[0] += 1
                ins.then_inc(step, 1)
                dve.wait_ge(step, n[0])

            link(nc.vector.memset(w_diag[:], 0.0))
            link(nc.vector.memset(filt[:], 0.0))
            for k in range(KU):
                link(nc.vector.memset(filt[0:1, k, 2 * KF + k:2 * KF + k + 1], 1.0))
            dve.wait_ge(pow_done, 1)
            link(nc.vector.tensor_tensor(filt[:, :, 0:KF], phi[:], sig[:, 2:3, :].to_broadcast([KI, NA, KF]), ALU.mult))
            link(nc.vector.tensor_tensor(filt[:, :, KF:2 * KF], filt[:, :, 0:KF],
                                         sgn_a[:].unsqueeze(2).to_broadcast([KI, NA, KF]), ALU.mult))
            dve.wait_ge(zeroed, 2)
            link(nc.vector.tensor_reduce(keep["peaks"][0:KI, 2:3], filt[:, :, 0:KF], mybir.AxisListType.XY,
                                         ALU.max, apply_absolute_value=True))
            nc.vector.memset(bn[:, 15:16], 0.0).then_inc(filt_ready, 1)

            dve.wait_ge(loaded["bn"], 128)
            dve.wait_ge(loaded["conv"], 32)
            link(nc.vector.tensor_reduce(bn[:, 4:5], w_raw[:], AX, ALU.add, apply_absolute_value=True))
            link(nc.vector.tensor_scalar(bn[:, 5:6], bn[:, 3:4], 1e-5, None, ALU.add))
            rsqrt_steps(nc, link, bn[:, 6:7], bn[:, 5:6], bn[:, 7:8], bn[:, 8:9])
            link(nc.vector.tensor_tensor(bn[:, 9:10], bn[:, 6:7], bn[:, 0:1], ALU.mult))
            link(nc.vector.scalar_tensor_tensor(keep["bn"][:, 0:1], bn[:, 4:5], 1.0 / (9 * CH), bn[:, 9:10],
                                                ALU.mult, ALU.mult))
            link(nc.vector.tensor_tensor(bn[:, 10:11], bn[:, 2:3], bn[:, 9:10], ALU.mult))
            link(nc.vector.tensor_tensor(keep["bn"][:, 1:2], bn[:, 1:2], bn[:, 10:11], ALU.subtract))
            for c in range(4):
                dve.wait_ge(filt_dft, c + 1)
                nc.vector.tensor_copy(filt_z[:, 8 * c:8 * c + 8, :].rearrange("p a k -> p (a k)"),
                                      p_f[:, c, 0:8 * NK]).then_inc(filt_saved, 1)

            dve.wait_ge(turned, 1)
            link(nc.vector.tensor_copy(keep["conv_w"][:].rearrange("p t o -> p (t o)"),
                                       p_w[:, 0:3, :].rearrange("p a b -> p (a b)")[:, 0:9 * 128]))

            dve.wait_ge(loaded["mix"], 32)
            link(nc.vector.tensor_tensor(mix[:, 8:12], mix[:, 0:4], mix[:, 4:8], ALU.add))
            link(nc.vector.tensor_reduce(mix[:, 16:17], mix[:, 8:12], AX, ALU.max))
            nc.vector.tensor_scalar(mix[:, 12:16], mix[:, 8:12], mix[:, 16:17], None, ALU.subtract).then_inc(exp_in, 1)
            dve.wait_ge(exp_done, 1)
            link(nc.vector.tensor_reduce(mix[:, 17:18], mix[:, 12:16], AX, ALU.add))
            link(nc.vector.reciprocal(mix[:, 18:19], mix[:, 17:18]))
            link(nc.vector.tensor_scalar(mix[:, 20:24], mix[:, 12:16], mix[:, 18:19], None, ALU.mult))
            link(nc.vector.tensor_reduce(mix[:, 19:20], mix[:, 20:24], AX, ALU.max))
            link(nc.vector.tensor_scalar(mix[:, 24:28], mix[:, 20:24], mix[:, 19:20], None, ALU.is_ge))
            link(nc.vector.tensor_scalar(mix[:, 28:32], mix[:, 24:28], -1.0, 1.0, ALU.mult, ALU.add))
            hard, soft, weight = mix[:, 32:36], mix[:, 20:24], mix[:, 36:40]
            link(nc.vector.tensor_copy(mix[:, 32:36], mix[:, 24:28]))
            for i in range(1, NBR):
                for j in range(i):
                    link(nc.vector.tensor_tensor(mix[:, 32 + i:33 + i], mix[:, 32 + i:33 + i], mix[:, 28 + j:29 + j],
                                                 ALU.mult))
            link(nc.vector.tensor_tensor(mix[:, 40:44], hard, soft, ALU.subtract))
            link(nc.vector.tensor_tensor(weight, mix[:, 40:44], soft, ALU.add))

            dve.wait_ge(loaded["mask"], 48)
            dve.wait_ge(loaded["step1"], 16)
            for i in range(NBR):
                mc = mask_col[:].rearrange("b (g i) -> b g i", i=NBR)[:, :, i]
                if i == 0:
                    link(nc.vector.tensor_scalar(mask_cs[:], mc, hard[0:NB, 0:1], None, ALU.mult))
                    link(nc.vector.tensor_scalar(mask_rs[:], mask_row[:, :, 0, :], hard[:, 0:1], None, ALU.mult))
                else:
                    link(nc.vector.scalar_tensor_tensor(mask_cs[:], mc, hard[0:NB, i:i + 1], mask_cs[:],
                                                        ALU.mult, ALU.add))
                    link(nc.vector.scalar_tensor_tensor(mask_rs[:], mask_row[:, :, i, :], hard[:, i:i + 1], mask_rs[:],
                                                        ALU.mult, ALU.add))
            for g in range(NMASK):
                link(nc.vector.tensor_scalar(keep["step1"][:, g, :], s1[:], mask_cs[:, g:g + 1], None, ALU.mult))
                link(nc.vector.tensor_tensor(keep["last"][:, g, :], s2[:], mask_rs[:, g, :], ALU.mult))

            dve.wait_ge(loaded["sel"], 16 * 2 * len(M_PIECES))
            for t, at, rows, _ in M_PIECES:
                p, w_row = slice(at, at + rows), keep["w_row"][at:at + rows, t:t + 1]
                link(nc.vector.tensor_tensor(branch[t][p, :], branch[t][p, :], weight[p, :], ALU.mult))
                link(nc.vector.tensor_reduce(w_row, branch[t][p, :], AX, ALU.add))
                link(nc.vector.tensor_scalar(keep["select"][t][p, :], select[t][p, :], w_row, None, ALU.mult))


def norm_and_convolve(nc, d, keep):
    with ExitStack() as own:
        def sb(name, shape, dt=F32):
            return own.enter_context(nc.sbuf_tensor(name, shape, dt))

        def sem(name):
            return own.enter_context(nc.semaphore(name))

        x_in, x_loaded = keep["x_in"], keep["x_loaded"]
        x_cen = sb("x_cen", [128, TOK])
        conv_y = sb("conv_y", [128, TOK])
        xc_t = sb("xc_t", [NB, NTOK, TW])
        sq1 = sb("sq1", [NB, NTOK, TW])
        x1_t = sb("x1_t", [NB, NTOK, TW])
        u_t = [sb(f"u_t{i}", [NB, NTOK, TW]) for i in range(2)]
        sq2 = sb("sq2", [NB, NTOK, TW])
        z_sb, z_stored = keep["z_sb"], keep["z_stored"]
        st1 = sb("st1", [NB, 5, 64])
        st2 = sb("st2", [NB, 8, 64])
        pad = keep["pad"]

        p_cen = own.enter_context(nc.psum_tensor("p_cen", [128, 2, 512], F32))
        p_conv = own.enter_context(nc.psum_tensor("p_conv", [128, 2, 512], F32))
        p_xt = own.enter_context(nc.psum_tensor("p_xt", [128, 2, 512], F32))
        p_rt = own.enter_context(nc.psum_tensor("p_rt", [128, 2, 512], F32))

        peaks_done, row_peak_done = sem("peaks_done"), sem("row_peak_done")
        (cen_ready, cen_saved, conv_ready, xt_ready, rt_ready, z_ready, sign_done, xt_copied, xt_squared, z_saved,
         y_saved, r_done, sq2_done, sq2_done_late, u_done, ssq1_done, x1_done, u_centered, u_centered_late,
         mean2_done, ssq2_done, guess2_step, rstd2_step, x1_stored, step) = (
            sem(n) for n in (
                "cen_ready", "cen_saved", "conv_ready", "xt_ready", "rt_ready", "z_ready", "sign_done", "xt_copied",
                "xt_squared", "z_saved", "y_saved", "r_done", "sq2_done", "sq2_done_late", "u_done", "ssq1_done",
                "x1_done", "u_centered", "u_centered_late", "mean2_done", "ssq2_done", "guess2_step", "rstd2_step",
                "x1_stored", "norm_step"))
        sp_turn = sem("sp_turn")

        x_pairs = d["x"].rearrange("(q i) c h w -> q (i c) (h w)", i=2)
        block = own.enter_context(nc.Block())

        @block.sync
        def _(sp):
            def load(q, slot):
                sp.dma_start(x_in[slot][:], x_pairs[q]).then_inc(x_loaded[slot], 16)

            def store_z(q):
                sp.wait_ge(z_saved, NTOK * q + 2 * NTOK)
                after_wait(sp, sp_turn)
                sp.dma_start(d["z"][:, :, bass.ds(q * 128, 128)],
                             z_sb[:].rearrange("p c (a n) -> p (c a) n", n=128)).then_inc(z_stored, 16)

            def body(q, slot, use):
                if not known(q, 0, 1):
                    store_z(q - 2)
                sp.wait_ge(x1_done, NTOK * q + NTOK)
                after_wait(sp, sp_turn)
                sp.dma_start(d["x1"][q], x1_t[:].rearrange("p c n -> p (c n)")).then_inc(x1_stored, 16)
                if not known(q, NPAIR - 2, NPAIR - 1):
                    sp.wait_ge(xt_ready, NTOK * q + NTOK)
                    after_wait(sp, sp_turn)
                    sp.wait_ge(r_done, NCONV * q + NCONV)
                    after_wait(sp, sp_turn)
                    load(q + 2, slot)

            sp.sem_inc(z_stored, 16)
            two_by_two(sp, NPAIR, body, last_apart=2)
            store_z(NPAIR - 2)
            store_z(NPAIR - 1)
            sp.wait_ge(x1_stored, 16 * NPAIR)

        @block.tensor
        def _(pe):
            def step1(q, slot, after, c):
                if c == 0:
                    pe.wait_ge(sign_done, NCONV * after + NCONV)
                pe.wait_ge(z_saved, NTOK * q + NTOK + max(c - 1, 0))
                if c % 2 == 0:
                    pe.wait_ge(u_done, 4 * q + c // 2 + 1)
                nc.tensor.matmul(p_cen[:, c % 2, :], keep["step1"][:, c // 2, :], u_t[slot][:, c, :],
                                 start=True, stop=True).then_inc(z_ready, 1)

            def center(q, slot, use, c):
                if c == 0:
                    pe.wait_ge(x_loaded[slot], 16 * use)
                if c >= 2:
                    pe.wait_ge(sign_done, NCONV * q + c - 1)
                elif not known(q, 0, 1, 2) and c == 0:
                    pe.wait_ge(z_saved, NTOK * q - NTOK)
                elif not is_first(q) and c == 0:
                    pe.wait_ge(sign_done, NCONV * q)
                nc.tensor.matmul(p_cen[:, c % 2, 0:CW], keep["center"][:], x_in[slot][:, CW * c:CW * c + CW],
                                 start=True, stop=True).then_inc(cen_ready, 1)

            def turn(q, c):
                if c == 0:
                    pe.wait_ge(r_done, NCONV * q + NCONV)
                if not (is_first(q) and c < 2):
                    pe.wait_ge(x1_done, NTOK * q + c - 1)
                for j in range(ACH):
                    a = ACH * c + j
                    mm = nc.tensor.transpose(p_rt[0:NB, c % 2, 128 * j:128 * j + 128], conv_y[:, a:TOK:NA],
                                             keep["ident"][:])
                mm.then_inc(rt_ready, 1)

            def body(q, slot, use):
                if is_first(q):
                    for c in range(NCONV):
                        center(0, 0, 1, c)
                pe.wait_ge(cen_saved, NCONV * q + NCONV)
                for c in range(NTOK):
                    if not (is_first(q) and c < 2):
                        pe.wait_ge(xt_copied, NTOK * q + c - 1)
                        pe.wait_ge(xt_squared, NTOK * q + c - 1)
                    for j in range(ACH):
                        a = ACH * c + j
                        mm = nc.tensor.transpose(p_xt[0:NB, c % 2, 128 * j:128 * j + 128], x_cen[:, a:TOK:NA],
                                                 keep["ident"][:])
                    mm.then_inc(xt_ready, 1)
                    if not known(q, 0, 1):
                        step1(q - 2, slot, q, c)
                for c in range(NCONV):
                    pe.wait_ge(sign_done, NCONV * q + min(c + 2, NCONV))
                    if not (is_first(q) and c < 2):
                        pe.wait_ge(y_saved, NCONV * q + c - 1)
                    for t in range(9):
                        rows = slice(CROWS * c + t // 3, CROWS * c + t // 3 + CROWS)
                        mm = nc.tensor.matmul(p_conv[:, c % 2, 0:CW], keep["conv_w"][:, t, :],
                                              pad[:, rows, t % 3:t % 3 + WID], start=(t == 0), stop=(t == 8))
                    mm.then_inc(conv_ready, 1)
                last = known(q, NPAIR - 1)
                for c in range(NTOK + 2):
                    if c < NCONV and not last:
                        center(q + 1, 1 - slot, use + slot, c)
                    if c >= 2:
                        turn(q, c - 2)

            two_by_two(pe, NPAIR, body, last_apart=2)
            for q in (NPAIR - 2, NPAIR - 1):
                for c in range(NTOK):
                    step1(q, q % 2, NPAIR - 1, c)

        @block.scalar
        def _(act):
            def save_z(q, c):
                if c == 0:
                    act.wait_ge(z_stored, 16 * q + 16)
                act.wait_ge(z_ready, NTOK * q + c + 1)
                nc.scalar.activation(z_sb[:, c, :], p_cen[:, c % 2, :], ACT.Copy).then_inc(z_saved, 1)

            def square2(q, slot):
                act.wait_ge(u_centered, q + 1)
                if not is_first(q):
                    act.wait_ge(ssq2_done, 2 * q - 1)
                nc.scalar.activation(sq2[:, 0:HALF, :], u_t[slot][:, 0:HALF, :], ACT.Square).then_inc(sq2_done, 1)
                if known(q, NPAIR - 1):
                    act.wait_ge(u_centered_late, q + 1)
                    act.wait_ge(ssq2_done, 2 * q)
                    nc.scalar.activation(sq2[:, HALF:NTOK, :], u_t[slot][:, HALF:NTOK, :],
                                         ACT.Square).then_inc(sq2_done_late, 1)

            def signs(q):
                if not is_first(q):
                    act.wait_ge(conv_ready, NCONV * q)
                    act.wait_ge(xt_ready, NTOK * q)
                for c in range(NCONV):
                    act.wait_ge(cen_ready, NCONV * q + c + 1)
                    nc.scalar.activation(x_cen[:, CW * c:CW * c + CW], p_cen[:, c % 2, 0:CW],
                                         ACT.Copy).then_inc(cen_saved, 1)
                    nc.scalar.activation(pad[:, 1 + CROWS * c:1 + CROWS * c + CROWS, 1:1 + WID],
                                         p_cen[:, c % 2, 0:CW].rearrange("p (h w) -> p h w", w=WID),
                                         ACT.Sign).then_inc(sign_done, 1)

            def body(q, slot, use):
                if is_first(q):
                    signs(0)
                if not is_first(q):
                    act.wait_ge(x1_done, NTOK * q)
                for c in range(NTOK):
                    act.wait_ge(xt_ready, NTOK * q + c + 1)
                    nc.scalar.activation(xc_t[:, c, :], p_xt[0:NB, c % 2, :], ACT.Copy).then_inc(xt_copied, 1)
                    if not is_first(q) and c % 4 == 0:
                        act.wait_ge(ssq1_done, 2 * q + c // 4 - 1)
                    nc.scalar.activation(sq1[:, c, :], p_xt[0:NB, c % 2, :], ACT.Square).then_inc(xt_squared, 1)
                    if not known(q, 0, 1):
                        save_z(q - 2, c)
                if not is_first(q):
                    square2(q - 1, 1 - slot)
                    act.wait_ge(rt_ready, NTOK * q)
                for c in range(NCONV):
                    act.wait_ge(conv_ready, NCONV * q + c + 1)
                    nc.scalar.activation(conv_y[:, CW * c:CW * c + CW], p_conv[:, c % 2, 0:CW], ACT.Identity,
                                         bias=keep["bn"][:, 1:2], scale=keep["bn"][:, 0:1]).then_inc(y_saved, 1)
                if not known(q, NPAIR - 1):
                    signs(q + 1)

            act.sem_inc(z_saved, NTOK)
            two_by_two(act, NPAIR, body, last_apart=2)
            for c in range(NTOK):
                save_z(NPAIR - 2, c)
            square2(NPAIR - 1, (NPAIR - 1) % 2)
            for c in range(NTOK):
                save_z(NPAIR - 1, c)

        @block.gpsimd
        def _(pool):
            shape = "p c (g n) -> p (c g) n"

            def normed(q, slot):
                n = [0]

                def link(ins):
                    n[0] += 1
                    ins.then_inc(rstd2_step, 1)
                    pool.wait_ge(rstd2_step, REFINE_STEPS * q + n[0])

                pool.wait_ge(guess2_step, 4 * q + 4)
                rsqrt_refine(nc, link, st2[:, 3, :], st2[:, 6, :], st2[:, 7, :], st2[:, 5, :])
                assert n[0] == REFINE_STEPS
                for c in range(4):
                    v = u_t[slot][:, 2 * c:2 * c + 2, :].rearrange(shape, n=CH)
                    r = st2[:, 3, 16 * c:16 * c + 16].unsqueeze(2).to_broadcast([NB, 16, CH])
                    nc.gpsimd.tensor_tensor(v, v, r, ALU.mult).then_inc(u_done, 1)

            def body(q, slot, use):
                for c in range(NCONV):
                    pool.wait_ge(y_saved, NCONV * q + c + 1)
                    v = conv_y[:, CW * c:CW * c + CW]
                    nc.gpsimd.tensor_tensor(v, v, x_in[slot][:, CW * c:CW * c + CW], ALU.add).then_inc(r_done, 1)
                if not is_first(q):
                    normed(q - 1, 1 - slot)
                if known(q, NPAIR - 1):
                    return
                pool.wait_ge(mean2_done, q + 1)
                if not known(q, 0, 1):
                    pool.wait_ge(z_ready, NTOK * q - NTOK)
                nc.gpsimd.tensor_tensor(u_t[slot][:, HALF:NTOK, :].rearrange(shape, n=CH),
                                        x1_t[:, HALF:NTOK, :].rearrange(shape, n=CH),
                                        st2[:, 0, 32:64].unsqueeze(2).to_broadcast([NB, 32, CH]),
                                        ALU.subtract).then_inc(u_centered_late, 1)
                pool.wait_ge(u_centered_late, q + 1)
                if not is_first(q):
                    pool.wait_ge(ssq2_done, 2 * q)
                v = u_t[slot][:, HALF:NTOK, :]
                nc.gpsimd.tensor_tensor(sq2[:, HALF:NTOK, :], v, v, ALU.mult).then_inc(sq2_done_late, 1)

            nc.gpsimd.memset(st2[:, 7, :], 1.5)
            pool.wait_ge(peaks_done, len(M_PIECES))
            nc.gpsimd.partition_all_reduce(keep["peak"][:], keep["peaks"][:], 128, bass.bass_isa.ReduceOp.max)
            two_by_two(pool, NPAIR, body, last_apart=2)

        @block.vector
        def _(dve):
            STEPS = 1 + RSQRT_STEPS + 2 + 2

            def guess2(q):
                n = [0]

                def link(ins):
                    n[0] += 1
                    ins.then_inc(guess2_step, 1)
                    dve.wait_ge(guess2_step, 4 * q + n[0])

                for h in range(2):
                    dve.wait_ge((sq2_done, sq2_done_late)[h], q + 1)
                    nc.vector.tensor_reduce(st2[:, 1, 32 * h:32 * h + 32],
                                            sq2[:, 4 * h:4 * h + 4, :].rearrange("p c (g n) -> p (c g) n", n=CH),
                                            AX, ALU.add).then_inc(ssq2_done, 1)
                dve.wait_ge(ssq2_done, 2 * q + 2)
                if not is_first(q):
                    dve.wait_ge(u_done, 4 * q)
                link(nc.vector.tensor_scalar(st2[:, 2, :], st2[:, 1, :], 1.0 / CH, 1e-5, ALU.mult, ALU.add))
                link(nc.vector.tensor_scalar(st2[:, 6, :], st2[:, 2, :], -0.5, None, ALU.mult))
                rsqrt_guess(nc, link, st2[:, 3, :], st2[:, 2, :], st2[:, 4, :])

            def body(q, slot, use):
                first = is_first(q)
                n = [0]

                def link(ins):
                    n[0] += 1
                    ins.then_inc(step, 1)
                    dve.wait_ge(step, STEPS * q + n[0])

                for h in range(2):
                    dve.wait_ge(xt_squared, NTOK * q + 4 * h + 4)
                    nc.vector.tensor_reduce(st1[:, 0, 32 * h:32 * h + 32],
                                            sq1[:, 4 * h:4 * h + 4, :].rearrange("p c (g n) -> p (c g) n", n=CH),
                                            AX, ALU.add).then_inc(ssq1_done, 1)
                dve.wait_ge(ssq1_done, 2 * q + 2)
                link(nc.vector.tensor_scalar(st1[:, 1, :], st1[:, 0, :], 1.0 / CH, 1e-6, ALU.mult, ALU.add))
                rsqrt_steps(nc, link, st1[:, 2, :], st1[:, 1, :], st1[:, 3, :], st1[:, 4, :])
                dve.wait_ge(xt_copied, NTOK * q + NTOK)
                for h in range(2):
                    v = xc_t[:, 4 * h:4 * h + 4, :].rearrange("p c (g n) -> p (c g) n", n=CH)
                    link(nc.vector.tensor_tensor(v, v, st1[:, 2, 32 * h:32 * h + 32].unsqueeze(2)
                                                 .to_broadcast([NB, 32, CH]), ALU.mult))
                if not first:
                    guess2(q - 1)
                    dve.wait_ge(u_centered_late, q)
                    dve.wait_ge(x1_stored, 16 * q)
                for c in range(NTOK):
                    dve.wait_ge(rt_ready, NTOK * q + c + 1)
                    nc.vector.tensor_tensor(x1_t[:, c, :], xc_t[:, c, :], p_rt[0:NB, c % 2, :],
                                            ALU.add).then_inc(x1_done, 1)
                for h in range(2):
                    dve.wait_ge(x1_done, NTOK * q + 4 * h + 4)
                    link(nc.vector.tensor_reduce(st2[:, 0, 32 * h:32 * h + 32],
                                                 x1_t[:, 4 * h:4 * h + 4, :].rearrange("p c (g n) -> p (c g) n", n=CH),
                                                 AX, ALU.add))
                nc.vector.tensor_scalar(st2[:, 0, :], st2[:, 0, :], 1.0 / CH, None, ALU.mult).then_inc(mean2_done, 1)
                dve.wait_ge(mean2_done, q + 1)
                if not known(q, 0, 1):
                    dve.wait_ge(z_ready, NTOK * q - NTOK)
                shape = "p c (g n) -> p (c g) n"
                for h, done in ((0, u_centered), (1, u_centered_late))[0:2 if known(q, NPAIR - 1) else 1]:
                    nc.vector.tensor_tensor(u_t[slot][:, HALF * h:HALF * h + HALF, :].rearrange(shape, n=CH),
                                            x1_t[:, HALF * h:HALF * h + HALF, :].rearrange(shape, n=CH),
                                            st2[:, 0, 32 * h:32 * h + 32].unsqueeze(2).to_broadcast([NB, 32, CH]),
                                            ALU.subtract).then_inc(done, 1)
                assert n[0] == STEPS, n[0]

            dve.wait_ge(keep["m_loaded"], 16 * 3 * (NBR + 1))
            for n, (t, at, rows, _) in enumerate(M_PIECES):
                p = slice(at, at + rows)
                peak, w_row = keep["peaks"][p, t:t + 1], keep["w_row"][p, t:t + 1]
                nc.vector.tensor_reduce(peak, keep["m_raw"][t][p, :], AX, ALU.max,
                                        apply_absolute_value=True).then_inc(row_peak_done, 1)
                dve.wait_ge(row_peak_done, n + 1)
                nc.vector.scalar_tensor_tensor(peak, peak, w_row, w_row, ALU.mult, ALU.mult).then_inc(peaks_done, 1)
            two_by_two(dve, NPAIR, body, last_apart=2)
            q = NPAIR - 1
            guess2(q)
            n = [0]

            def link(ins):
                n[0] += 1
                ins.then_inc(rstd2_step, 1)
                dve.wait_ge(rstd2_step, REFINE_STEPS * q + n[0])

            rsqrt_newton(nc, link, st2[:, 3, :], st2[:, 2, :], st2[:, 4, :], st2[:, 5, :])
            dve.wait_ge(u_centered_late, NPAIR)
            for c in range(4):
                v = u_t[q % 2][:, 2 * c:2 * c + 2, :].rearrange("p c (g n) -> p (c g) n", n=CH)
                r = st2[:, 3, 16 * c:16 * c + 16].unsqueeze(2).to_broadcast([NB, 16, CH])
                nc.vector.tensor_tensor(v, v, r, ALU.mult).then_inc(u_done, 1)


PLAN = [("x", 4), ("t1", 4), ("h", 2), ("t2", 2), ("h", 2), ("t2", 2), ("h", 2), ("inv", 2), ("h", 2), ("inv", 2),
        ("mix", 4)]
TAIL = ("t1", "t2", "inv")
RING = 7


def unit_chunks():
    seen, out = {}, []
    for stage, count in PLAN:
        for _ in range(count):
            k = seen.get(stage, 0)
            seen[stage] = k + 1
            out.append((stage, k, len(out)))
    return out


def chunk_is_there(stage, u):
    return (u > 0) if stage in TAIL else (u < NUNIT)


def chunks_until(u, p, engine=None):
    plan = unit_chunks()
    if isinstance(u, int):
        return sum(1 for w in range(u + 1) for stage, _, at in plan
                   if chunk_is_there(stage, w) and (w < u or at <= p) and engine in (None, at % 2))
    per_unit = sum(1 for _, _, at in plan if engine in (None, at % 2))
    missing = sum(1 for stage, _, at in plan if stage in TAIL and engine in (None, at % 2))
    return per_unit * u - missing + sum(1 for _, _, at in plan if at <= p and engine in (None, at % 2))


def mix_frequencies(nc, d, keep):
    chunks = unit_chunks()
    NCH = len(chunks)
    assert NCH % RING == 0 and NCH % 2 == 0
    pos = {(s, k): p for s, k, p in chunks}
    with ExitStack() as own:
        def sb(name, shape, dt=F32):
            return own.enter_context(nc.sbuf_tensor(name, shape, dt))

        def sem(name):
            return own.enter_context(nc.semaphore(name))

        z_in = [sb(f"z_in{i}", [128, ZCOLS]) for i in range(2)]
        fwd = [sb(f"fwd{i}", [128, 128]) for i in range(2)]
        inv = [sb(f"inv{i}", [128, 2, 128]) for i in range(2)]
        xf = sb("xf", [128, NF, NIMG])
        hf = sb("hf", [128, NF, 2, CH])
        y1 = sb("y1", [128, 8, 2, 2, CH])
        y2 = sb("y2", [128, 16, 2, 2, NALPHA])
        yt = sb("yt", [128, 16, 2, CH])
        wf = sb("wf", [128, 2, 16, CH])
        v_mov = [sb(f"v_mov{i}", [KROWS, NF], F16) for i in range(2)]
        m_sta = [sb(f"m_sta{i}", [KROWS, CH, 128], F16) for i in range(2)]
        sc = sb("sc", [128, 12])
        ring = own.enter_context(nc.psum_tensor("ring", [128, RING, 512], F32))
        p_v = own.enter_context(nc.psum_tensor("p_v", [128, 512], F32))

        z_loaded = [sem(f"z_loaded{i}") for i in range(2)]
        inv_loaded = [sem(f"inv_loaded{i}") for i in range(2)]
        chunk_ready, v_ready, v_saved, w_stored, w_free = (
            sem(n) for n in ("chunk_ready", "v_ready", "v_saved", "w_stored", "w_free"))
        sp_turn, pool_turn = sem("sp_turn"), sem("pool_turn")
        m_ready, m_high_zeroed, m_low_zeroed, v_high, scaled, scale_step, reals_done = (
            sem(n) for n in (
                "m_ready", "m_high_zeroed", "m_low_zeroed", "v_high", "scaled", "scale_step", "reals_done"))
        m_saved = [sem("m_high_saved"), sem("m_low_saved")]
        M_CHUNKS = CH * CH // 512
        DCH = 512 // CH
        saved = [sem("saved_by_act"), sem("saved_by_dve")]

        z_units = d["z"].rearrange("(u r) a c -> u (r a) c", r=4)
        w_units = d["w"].rearrange("(u s r) a (h m) e -> u h (r a) s (m e)", s=2, r=2, h=2)
        block = own.enter_context(nc.Block())

        def out_of(stage, k, u_prev):
            def view(bank):
                if stage == "mix":
                    return (y1[:, 4 * (k % 2):4 * (k % 2) + 4, :, k // 2, :],
                            bank.rearrange("p (a r e) -> p a r e", r=2, e=CH))
                if stage == "t1":
                    r, part = divmod(k, 2)
                    return (y2[:, :, :, r, 16 * part:16 * part + 16].rearrange("p m h f -> p f h m"),
                            bank.rearrange("p (f h m) -> p f h m", h=2, m=16))
                if stage == "t2":
                    return yt[:, 4 * k:4 * k + 4, :, :].rearrange("p m s e -> p (m s e)"), bank
                g, s = divmod(k, 2)
                return wf[:, s, 8 * g:8 * g + 8, :].rearrange("p m e -> p (m e)"), bank
            return view

        @block.sync
        def _(sp):
            def load(u, slot):
                sp.dma_start(z_in[slot][:], z_units[u]).then_inc(z_loaded[slot], 16)
                sp.dma_start(fwd[slot][:], d["c_fwd"][u]).then_inc(z_loaded[slot], 16)

            def load_inv(u, slot):
                sp.dma_start(inv[slot][:].rearrange("p n f -> p (n f)"), d["c_inv"][u]).then_inc(inv_loaded[slot], 16)

            def body(u, slot, use):
                if not known(u, NUNIT - 1):
                    if not is_first(u):
                        sp.wait_ge(chunk_ready, chunks_until(u - 1, pos["mix", 3]))
                        after_wait(sp, sp_turn)
                    load(u + 1, 1 - slot)
                    if not is_first(u):
                        sp.wait_ge(chunk_ready, chunks_until(u, pos["inv", 3]))
                        after_wait(sp, sp_turn)
                    load_inv(u + 1, 1 - slot)

            def load_x1(n):
                q, tile = PREFETCHED[n], keep["x1_early"][n]
                sp.dma_start(tile[0:NB].rearrange(keep["x1_shapes"][n]), d["x1"][q]
                             ).then_inc(keep["x1_early_loaded"], 16)

            load_inv(0, 0)
            sp.wait_ge(keep["z_stored"], 16 * NPAIR + 16)
            load(0, 0)
            body(0, 0, 1)
            body(1, 1, 1)
            for e in range(2):
                sp.wait_ge(m_saved[e], 2 * M_CHUNKS)
            for n in range(len(PREFETCHED)):
                load_x1(n)
            with sp.Fori(1, NUNIT // 2 - 1) as h:
                body(2 * h, 0, h + 1)
                body(2 * h + 1, 1, h + 1)
            for u in (NUNIT - 2, NUNIT - 1):
                body(u, u % 2, u // 2 + 1)

        @block.gpsimd
        def _(pool):
            def store(u):
                for e in range(2):
                    pool.wait_ge(saved[e], chunks_until(u + 1, pos["inv", 3], e))
                after_wait(pool, pool_turn)
                for h in range(2):
                    nc.gpsimd.dma_start(w_units[u, h], wf[64 * h:64 * h + 64].rearrange("p s m e -> p s (m e)")
                                        ).then_inc(w_stored, 16)
                pool.wait_ge(w_stored, 32 * (u + 1))
                pool.sem_inc(w_free, 1)

            pool.sem_inc(w_free, 1)
            nc.gpsimd.memset(m_sta[1][:].rearrange("k e n -> k (e n)").bitcast(F32), 0.0).then_inc(m_low_zeroed, 1)
            for part in v_mov:
                nc.gpsimd.memset(part[:].bitcast(F32), 0.0).then_inc(m_low_zeroed, 1)

            store(0)
            with pool.Fori(1, NUNIT - 1) as u:
                store(u)
            store(NUNIT - 1)

        def bank_free(eng, u, p):
            if not isinstance(u, int):
                w, at = (u, p - RING) if p >= RING else (u - 1, p - RING + NCH)
                eng.wait_ge(saved[at % 2], chunks_until(w, at, at % 2))
                return
            before = [(w, at) for w in range(u + 1) for stage, _, at in chunks
                      if chunk_is_there(stage, w) and at % RING == p % RING and (w < u or at < p)]
            if before:
                w, at = before[-1]
                eng.wait_ge(saved[at % 2], chunks_until(w, at, at % 2))

        def all_saved(eng, u, p):
            for e in range(2):
                eng.wait_ge(saved[e], chunks_until(u, p, e))

        @block.tensor
        def _(pe):
            def unit(u, slot, use, head, tail):
                if head:
                    pe.wait_ge(z_loaded[slot], 32 * use)
                    if not is_first(u):
                        pe.wait_ge(v_saved, 2 * u)
                    lhs = z_in[slot][:, NIMG * CH:ZCOLS]
                    nc.tensor.matmul(p_v[0:NK, 0:NF], lhs, fwd[slot][:, 0:NF], start=True, stop=True)
                    nc.tensor.matmul(p_v[KI:KROWS, 0:NF], lhs, fwd[slot][:, NF:2 * NF], start=True,
                                     stop=True).then_inc(v_ready, 1)
                for stage, k, p in chunks:
                    if not (tail if stage in TAIL else head):
                        continue
                    bank_free(pe, u, p)
                    bank = ring[:, p % RING, :]
                    if stage == "x":
                        for j in range(4):
                            at = CH * (8 * k + 2 * j)
                            mm = nc.tensor.matmul(bank[:, 128 * j:128 * j + 128], z_in[slot][:, at:at + 2 * CH],
                                                  fwd[slot][:], start=True, stop=True)
                    elif stage == "h":
                        if k == 0:
                            pe.wait_ge(v_saved, 2 * u + 2)
                        for i in range(8):
                            for n, (m, v) in enumerate(((0, 0), (0, 1), (1, 0))):
                                mm = nc.tensor.matmul(bank[:, NF * i:NF * i + NF], m_sta[m][:, 8 * k + i, :],
                                                      v_mov[v][:], start=(n == 0), stop=(n == 2))
                    elif stage == "mix":
                        if k == 0:
                            all_saved(pe, u, pos["h", 7])
                            if is_first(u):
                                pe.wait_ge(reals_done, 3)
                        for i in range(4):
                            for j in range(4):
                                f = 16 * k + 4 * i + j
                                mm = nc.tensor.matmul(bank[32 * j:32 * j + 32, 128 * i:128 * i + 128], xf[:, f, :],
                                                      hf[:, f, :, :].rearrange("p r e -> p (r e)"),
                                                      start=True, stop=True, tile_position=(0, 32 * j))
                    elif stage == "t1":
                        if k == 0:
                            all_saved(pe, u - 1, pos["mix", 3])
                        r, part = divmod(k, 2)
                        for i in range(4):
                            mm = nc.tensor.transpose(bank[:, 128 * i:128 * i + 128],
                                                     y1[:, 4 * part + i, r, :, :].rearrange("p s e -> p (s e)"),
                                                     keep["ident"][:])
                    elif stage == "t2":
                        if k == 0:
                            all_saved(pe, u, pos["t1", 3])
                        for i in range(4):
                            mm = nc.tensor.transpose(bank[:, 128 * i:128 * i + 128],
                                                     y2[:, 4 * k + i, :, :, :].rearrange("p h r f -> p (h r f)"),
                                                     keep["ident"][:])
                    else:
                        g, s = divmod(k, 2)
                        if s == 0:
                            all_saved(pe, u, pos["t2", 2 * g + 1])
                        if k == 0:
                            pe.wait_ge(inv_loaded[1 - slot], 16 * (use if slot else use - 1))
                        mm = nc.tensor.matmul(bank, inv[1 - slot][:, s, :], yt[:, 8 * g:8 * g + 8, s, :],
                                              start=True, stop=True)
                    mm.then_inc(chunk_ready, 1)

            def body(u, slot, use):
                unit(u, slot, use, True, not is_first(u))

            for c in range(M_CHUNKS):
                if c >= RING:
                    for e in range(2):
                        pe.wait_ge(m_saved[e], 2 * (c - RING + 1))
                half, at = divmod(512 * c, M_COLS // 2)
                last = slice(KI * half, KI * half + ROWS_B)
                nc.tensor.matmul(ring[0:KROWS, c % RING, :], keep["select"][0][:],
                                 keep["m_raw"][0][:, 512 * c:512 * c + 512], start=True, stop=False)
                mm = nc.tensor.matmul(ring[0:KROWS, c % RING, :], keep["select"][1][last, :],
                                      keep["m_raw"][1][last, at:at + 512], start=False, stop=True)
                mm.then_inc(m_ready, 1)
            for e in range(2):
                pe.wait_ge(m_saved[e], 2 * M_CHUNKS)

            two_by_two(pe, NUNIT, body)
            unit(NUNIT, 0, NUNIT // 2 + 1, False, True)

        def m_part(n, copy_of, c):
            at = KI * copy_of
            return (m_sta[n][at:at + NK, :, CH * copy_of + DCH * c:CH * copy_of + DCH * c + DCH]
                    .rearrange("k e d -> k d e"),
                    ring[at:at + NK, c % RING, :].rearrange("k (d e) -> k d e", e=CH))

        def saver(eng, which, copy):
            mine = [(stage, k) for stage, k, p in chunks if p % 2 == which]
            first_inv = min(k for stage, k in mine if stage == "inv")
            last_h = max(k for stage, k in mine if stage == "h")

            def unit(u, head, tail):
                if head and which:
                    eng.wait_ge(v_ready, u + 1)
                    for at in (0, KI):
                        nc.vector.tensor_scalar(v_mov[0][at:at + NK, :], p_v[at:at + NK, 0:NF],
                                                sc[at:at + NK, V_SCALE:V_SCALE + 1], None, ALU.mult).then_inc(v_high, 1)
                    eng.wait_ge(v_high, 2 * u + 2)
                    for at in (0, KI):
                        nc.vector.scalar_tensor_tensor(v_mov[1][at:at + NK, :], p_v[at:at + NK, 0:NF],
                                                       sc[at:at + NK, V_SCALE:V_SCALE + 1], v_mov[0][at:at + NK, :],
                                                       ALU.mult, ALU.subtract).then_inc(v_saved, 1)
                for stage, k, p in chunks:
                    if p % 2 != which or not (tail if stage in TAIL else head):
                        continue
                    eng.wait_ge(chunk_ready, chunks_until(u, p))
                    bank = ring[:, p % RING, :]
                    if (stage, k) == ("inv", first_inv):
                        eng.wait_ge(w_free, u)
                    if stage == "x":
                        src = bank.rearrange("p (j r f) -> p r j f", r=2, f=NF)
                        for i, r in ((0, 0), (0, 1), (1, 0), (1, 1)):
                            ins = copy(xf[CH * r:CH * r + CH, :, 8 * k + i:8 * k + 8:2].rearrange("p f j -> p j f"),
                                       src[CH * i:CH * i + CH, r])
                        ins.then_inc(saved[which], 1)
                    elif stage == "h":
                        src = bank.rearrange("p (e f) -> p e f", f=NF)
                        e8 = slice(8 * k, 8 * k + 8)
                        copy(hf[:, :, 0, e8].rearrange("p f e -> p e f"), src)
                        copy(hf[0:CH, :, 1, e8].rearrange("p f e -> p e f"), src[CH:2 * CH], -1.0)
                        copy(hf[CH:2 * CH, :, 1, e8].rearrange("p f e -> p e f"), src[0:CH]).then_inc(saved[which], 1)
                    else:
                        dst, src = out_of(stage, k, u)(bank)
                        copy(dst, src).then_inc(saved[which], 1)
                    if is_first(u) and which and (stage, k) == ("h", last_h):
                        for e in range(2):
                            eng.wait_ge(saved[e], chunks_until(u, pos["h", 7], e))
                        nc.vector.tensor_scalar(hf[CH:2 * CH, 0, 1, :], hf[CH:2 * CH, 0, 0, :], -1.0, None,
                                                ALU.mult).then_inc(reals_done, 1)
                        nc.vector.memset(hf[0:CH, 0, 1, :], 0.0).then_inc(reals_done, 1)
                        eng.wait_ge(reals_done, 1)
                        nc.vector.memset(hf[CH:2 * CH, 0, 0, :], 0.0).then_inc(reals_done, 1)

            return unit

        M_SCALE, V_SCALE, UNSCALE = 8, 9, 10

        @block.scalar
        def _(act):
            def copy(dst, src, scale=1.0):
                return nc.scalar.activation(dst, src, ACT.Copy, scale=scale)

            act.wait_ge(m_high_zeroed, 1)
            act.wait_ge(scaled, 1)
            for c in range(M_CHUNKS):
                act.wait_ge(m_ready, c + 1)
                for copy_of in range(2):
                    dst, src = m_part(0, copy_of, c)
                    scale = sc[KI * copy_of:KI * copy_of + NK, M_SCALE:M_SCALE + 1]
                    nc.scalar.activation(dst, src, ACT.Copy, scale=scale).then_inc(m_saved[0], 1)
            unit = saver(act, 0, copy)
            two_by_two(act, NUNIT, lambda u, slot, use: unit(u, True, not is_first(u)))
            unit(NUNIT, False, True)

        @block.vector
        def _(dve):
            def copy(dst, src, scale=None):
                if scale is None:
                    return nc.vector.tensor_copy(dst, src)
                return nc.vector.tensor_scalar(dst, src, scale, None, ALU.mult)

            n = [0]

            def link(ins):
                n[0] += 1
                ins.then_inc(scale_step, 1)
                dve.wait_ge(scale_step, n[0])

            nc.vector.memset(m_sta[0][:].rearrange("k e n -> k (e n)").bitcast(F32), 0.0).then_inc(m_high_zeroed, 1)
            link(nc.vector.tensor_tensor(sc[:, 0:1], keep["peak"][:, 0:1], keep["peak"][:, 1:2], ALU.max))
            link(nc.vector.tensor_scalar(sc[:, 1:2], keep["peak"][:, 2:3], float(PHI_LEN), 1.0, ALU.mult, ALU.max))
            link(nc.vector.tensor_scalar(sc[:, 0:1], sc[:, 0:1], 2.0 * NBR, 1e-30, ALU.mult, ALU.max))
            link(nc.vector.tensor_scalar(sc[:, 2:4].bitcast(I32), sc[:, 0:2].bitcast(I32), EXPONENT, None,
                                         ALU.bitwise_and))
            link(nc.vector.tensor_scalar(sc[:, 8:10].bitcast(I32), sc[:, 2:4].bitcast(I32), -1.0,
                                         float((2 * 127 + HALF_TOP) << 23), ALU.mult, ALU.add))
            nc.vector.memset(sc[:, 11:12], 0.0).then_inc(scaled, 1)
            link(nc.vector.scalar_tensor_tensor(sc[:, 10:11], sc[:, 2:3], 2.0 ** (-2 * HALF_TOP), sc[:, 3:4],
                                                ALU.mult, ALU.mult))
            link(nc.vector.tensor_scalar(keep["last"][:], keep["last"][:], sc[:, UNSCALE:UNSCALE + 1], None, ALU.mult))
            dve.wait_ge(m_low_zeroed, 3)
            for c in range(M_CHUNKS):
                dve.wait_ge(m_saved[0], 2 * c + 2)
                for copy_of in range(2):
                    dst, src = m_part(1, copy_of, c)
                    nc.vector.scalar_tensor_tensor(dst, src, sc[KI * copy_of:KI * copy_of + NK, M_SCALE:M_SCALE + 1],
                                                   m_part(0, copy_of, c)[0], ALU.mult, ALU.subtract
                                                   ).then_inc(m_saved[1], 1)
            unit = saver(dve, 1, copy)
            two_by_two(dve, NUNIT, lambda u, slot, use: unit(u, True, not is_first(u)))
            unit(NUNIT, False, True)


def finish(nc, d, keep):
    with ExitStack() as own:
        def sb(name, shape, dt=F32):
            return own.enter_context(nc.sbuf_tensor(name, shape, dt))

        def sem(name):
            return own.enter_context(nc.semaphore(name))

        w_in = [sb(f"w_in{i}", [NROW, NA, 128]) for i in range(2)]
        x1_in = [sb(f"x1_in{i}", [NB, NA, 128]) for i in range(2)]
        out_sb = [sb(f"out_sb{i}", [128, NB, NA]) for i in range(2)]
        p_out = own.enter_context(nc.psum_tensor("p_out", [128, 4, 512], F32))
        p_x1 = own.enter_context(nc.psum_tensor("p_x1", [128, 4, 512], F32))
        w_loaded = [sem(f"w_loaded{i}") for i in range(2)]
        x1_loaded = [sem(f"x1_loaded{i}") for i in range(2)]
        out_stored = [sem(f"out_stored{i}") for i in range(2)]
        out_ready, x1_ready, x1_saved, summed = (sem(n) for n in ("out_ready", "x1_ready", "x1_saved", "out_summed"))
        sp_turn, pool_turn = sem("sp_turn"), sem("pool_turn")
        w_rows = d["w"].rearrange("r a i e -> r a (i e)")
        out_pairs = d["out"].rearrange("(q i) c h w -> q (i c) (h w)", i=2)
        BANKS = 4
        block = own.enter_context(nc.Block())

        def tokens(slot, c):
            return out_sb[slot][:, :, ACH * c:ACH * c + ACH].rearrange("p b a -> p a b")

        def view(bank):
            return bank[:, 0:ACH * NB].rearrange("p (a b) -> p a b", b=NB)

        @block.sync
        def _(sp):
            def load_w(q, slot):
                sp.dma_start(w_in[slot][:], w_rows[:, :, bass.ds(q * 128, 128)]).then_inc(w_loaded[slot], 16)

            def load_x1(q, slot):
                sp.dma_start(x1_in[slot][:].rearrange("p a n -> p (a n)"), d["x1"][q]).then_inc(x1_loaded[slot], 16)

            def body(q, slot, use):
                if known(q, NPAIR - 1):
                    return
                if not is_first(q):
                    sp.wait_ge(out_ready, NTOK * q)
                    after_wait(sp, sp_turn)
                load_w(q + 1, 1 - slot)
                if is_first(q):
                    load_x1(2, 0)
                    load_x1(3, 1)
                elif not known(q + 1, 2, 3, *PREFETCHED):
                    load_x1(q + 1, 1 - slot)

            load_w(0, 0)
            for q in range(4):
                body(q, q % 2, q // 2 + 1)
            with sp.Fori(2, NPAIR // 2 - 2) as h:
                body(2 * h, 0, h + 1)
                body(2 * h + 1, 1, h + 1)
            for q in range(NPAIR - 4, NPAIR):
                body(q, q % 2, q // 2 + 1)

        @block.gpsimd
        def _(pool):
            def body(q, slot, use):
                pool.wait_ge(summed, NTOK * q + NTOK)
                after_wait(pool, pool_turn)
                nc.gpsimd.dma_start(out_pairs[q], out_sb[slot][:].rearrange("p b a -> p (b a)")
                                    ).then_inc(out_stored[slot], 16)

            two_by_two(pool, NPAIR, body)
            for s in range(2):
                pool.wait_ge(out_stored[s], 16 * (NPAIR // 2))

        @block.tensor
        def _(pe):
            def body(q, slot, use):
                if known(q, *PREFETCHED):
                    n = PREFETCHED.index(q)
                    pe.wait_ge(keep["x1_early_loaded"], 16 * len(PREFETCHED))
                    x1 = keep["x1_early"][n][0:NB].rearrange(keep["x1_shapes"][n]).rearrange("p (a n) -> p a n", a=NA)
                else:
                    pe.wait_ge(x1_loaded[slot], 16 * (use - 1))
                    x1 = x1_in[slot]
                for c in range(NTOK):
                    if not (is_first(q) and c < BANKS):
                        pe.wait_ge(x1_saved, NTOK * q + c + 1 - BANKS)
                    for j in range(ACH):
                        mm = nc.tensor.transpose(p_x1[:, c % BANKS, NB * j:NB * j + NB], x1[:, ACH * c + j, :],
                                                 keep["ident"][0:NB, 0:NB])
                    mm.then_inc(x1_ready, 1)
                    if not (is_first(q) and c < BANKS):
                        pe.wait_ge(summed, NTOK * q + c + 1 - BANKS)
                    if c == 0:
                        pe.wait_ge(w_loaded[slot], 16 * use)
                    for j in range(ACH):
                        a = ACH * c + j
                        mm = nc.tensor.matmul(p_out[:, c % BANKS, NB * j:NB * j + NB], w_in[slot][:, a, :],
                                              keep["last"][:, a // MASKG, :], start=True, stop=True)
                    mm.then_inc(out_ready, 1)

            two_by_two(pe, NPAIR, body, last_apart=2)

        @block.scalar
        def _(act):
            def body(q, slot, use):
                if not known(q, 0, 1):
                    act.wait_ge(out_stored[slot], 16 * (use - 1))
                for c in range(NTOK):
                    act.wait_ge(x1_ready, NTOK * q + c + 1)
                    nc.scalar.activation(tokens(slot, c), view(p_x1[:, c % BANKS, :]), ACT.Copy).then_inc(x1_saved, 1)

            two_by_two(act, NPAIR, body)

        @block.vector
        def _(dve):
            def body(q, slot, use):
                for c in range(NTOK):
                    dve.wait_ge(x1_saved, NTOK * q + c + 1)
                    dve.wait_ge(out_ready, NTOK * q + c + 1)
                    to = tokens(slot, c)
                    nc.vector.tensor_tensor(to, view(p_out[:, c % BANKS, :]), to, ALU.add).then_inc(summed, 1)

            two_by_two(dve, NPAIR, body)


def build(nc, d):
    d["z"] = nc.dram_tensor("z_scratch", [NROW, NA, ZCOLS], F32).ap()
    d["w"] = nc.dram_tensor("w_scratch", [NROW, NA, NIMG, CH], F32).ap()
    d["x1"] = nc.dram_tensor("x1_scratch", [NPAIR, NB, NA * 128], F32).ap()
    with ExitStack() as ctx:
        def sb(name, shape, dt=F32):
            return ctx.enter_context(nc.sbuf_tensor(name, shape, dt))

        keep = {
            "ident": sb("ident", [128, 128]),
            "center": sb("center", [128, 128]),
            "bn": sb("bn_scale_bias", [128, 2]),
            "conv_w": sb("conv_w", [128, 9, 128], BF16),
            "step1": sb("step1_masked", [NB, NMASK, NROW]),
            "last": sb("last_masked", [NROW, NMASK, NB]),
            "m_raw": [sb("m_raw_a", [ROWS_A, M_COLS]), sb("m_raw_b", [KROWS, M_COLS // 2])],
            "select": [sb("select_weighted_a", [ROWS_A, KROWS]), sb("select_weighted_b", [KROWS, KROWS])],
            "w_row": sb("w_row", [ROWS_A, 2]),
            "peaks": sb("peaks", [128, 3]),
            "peak": sb("peak", [128, 3]),
            "m_loaded": ctx.enter_context(nc.semaphore("m_loaded")),
            "z_sb": sb("z_sb", [NROW, NTOK, TW]),
            "z_stored": ctx.enter_context(nc.semaphore("z_stored")),
            "x1_early_loaded": ctx.enter_context(nc.semaphore("x1_early_loaded")),
        }
        with ExitStack() as early:
            keep["x_in"] = [early.enter_context(nc.sbuf_tensor(f"x_in{i}", [128, TOK], F32)) for i in range(2)]
            keep["x_loaded"] = [early.enter_context(nc.semaphore(f"x_loaded{i}")) for i in range(2)]
            keep["pad"] = early.enter_context(nc.sbuf_tensor("signs_padded", [128, HGT + 2, WID + 2], BF16))
            prepare(nc, d, keep)
            norm_and_convolve(nc, d, keep)
        keep["x1_early"] = [keep["m_raw"][0], keep["z_sb"]] + [sb(f"x1_early{i}", [NB, NA * 128]) for i in range(2)]
        keep["x1_shapes"] = ["p n -> p n", "p c n -> p (c n)", "p n -> p n", "p n -> p n"]
        mix_frequencies(nc, d, keep)
        finish(nc, d, keep)


_INS = {
    "x": "x", "L0_conv_weight": "weight", "L0_conv_gamma": "gamma", "L0_conv_beta": "beta",
    "L0_conv_bn_mean": "bn_mean", "L0_conv_bn_var": "bn_var", "L0_ffn_sigma": "sigma", "L0_ffn_phi": "phi",
    "L0_ffn_M_u": "M_u", "L0_ffn_M_phi_plus": "M_plus", "L0_ffn_M_phi_minus": "M_minus",
    "L0_ffn_log_weights": "log_weights", "L0_ffn_gumbel": "gumbel",
}


def kernel(**inputs):
    import concourse.bacc as _bacc
    from concourse.bass_utils import run_bass_kernel_spmd as _run

    nc = _bacc.Bacc("TRN2", target_bir_lowering=False, num_devices=1)
    arrays, d = {}, {}
    given = {short: np.ascontiguousarray(inputs[name]) for name, short in _INS.items()}
    for name, a in {**given, **constants()}.items():
        arrays["in_" + name] = a
        d[name] = nc.dram_tensor("in_" + name, a.shape, mybir.dt.from_np(a.dtype), kind="ExternalInput").ap()
    d["out"] = nc.dram_tensor("out_dram", given["x"].shape, F32, kind="ExternalOutput").ap()
    build(nc, d)
    r = _run(nc, [arrays], core_ids=[0])
    return r.results[0]["out_dram"]
```
